# Optimizing a Trainium2 kernel written in Bass

```python
import numpy as np
import jax
import jax.numpy as jnp

def _softmax(x, axis=-1):
    return jax.nn.softmax(x, axis=axis)
def _gelu(x):
    return jax.nn.gelu(x, approximate=True)
def _silu(x):
    return jax.nn.silu(x)
def _sigmoid(x):
    return jax.nn.sigmoid(x)
def _layernorm(x, axis=-1, eps=1e-5):
    m = jnp.mean(x, axis=axis, keepdims=True)
    v = jnp.var(x, axis=axis, keepdims=True)
    return (x - m) / jnp.sqrt(v + eps)
def _scatter_add(tgt, idx, src, axis=0):
    return tgt.at[idx].add(src)
def _segment_sum(src, seg, n):
    return jax.ops.segment_sum(src, seg, n)

kernel_name = 'mk_conv_preact_d2_conv_nchw64_7ad1c0'

def setup_inputs(seed: int = 0):
    np.random.seed(seed)
    _w = jnp.asarray
    def _rec_inputs():
        import jax
        import jax.numpy as jnp
        _gk = jax.random.key(seed)
        x = -7.109e-05 + 0.9999 * jax.random.normal(jax.random.fold_in(_gk, 1), (16, 64, 256, 256), jnp.float32)
        return x
    x = _rec_inputs()
    def _L0_conv_setup():
        import jax, jax.numpy as jnp
        import numpy as np
        N_HEADS = 4
        key = jax.random.key(seed)
        k1, k2, k3 = jax.random.split(key, 3)
        x = jax.random.normal(k1, (16, 64, 256, 256), dtype=jnp.float32)
        weight_re = jax.random.normal(k2, (4, 16, 16, 32, 17), dtype=jnp.float32) * 0.01
        weight_im = jax.random.normal(k3, (4, 16, 16, 32, 17), dtype=jnp.float32) * 0.01
        bias = jnp.zeros((64, 1, 1), dtype=jnp.float32)
        return {'x': x, 'weight_re': weight_re, 'weight_im': weight_im, 'bias': bias}
    _L0_conv_all = _L0_conv_setup()
    _L0_conv_in = {k: v for k, v in _L0_conv_all.items() if k in ('weight_re', 'weight_im', 'bias', )}
    del _L0_conv_all

    def _L1_conv_setup():
        import jax, jax.numpy as jnp
        import numpy as np
        M_PER_GROUP = 16
        EPS = 0.001
        key = jax.random.key(seed)
        x = jax.random.normal(key, (32, 64, 64, 256), dtype=jnp.float32)
        return {'x': x}
    _L1_conv_all = _L1_conv_setup()
    _L1_conv_in = {k: v for k, v in _L1_conv_all.items() if k in ()}
    del _L1_conv_all

    return {
        "x": x,
        "L0_conv_weight_re": _L0_conv_in["weight_re"],
        "L0_conv_weight_im": _L0_conv_in["weight_im"],
        "L0_conv_bias": _L0_conv_in["bias"],
    }

def reference(x, L0_conv_weight_re, L0_conv_weight_im, L0_conv_bias):
    import jax
    import jax.numpy as jnp
    def _L0_conv_ref(x, weight_re, weight_im, bias):
        import jax, jax.numpy as jnp
        import numpy as np
        N_HEADS = 4
        B, C, H, W = x.shape
        weight = weight_re + 1j * weight_im
        n_heads = weight.shape[0]
        head_in = C // n_heads
        head_out = weight.shape[2]
        x_freq = jnp.fft.rfft2(x, axes=(-2, -1))
        fH, fW = (x_freq.shape[-2], x_freq.shape[-1])
        m_x = min(weight.shape[-2], fH)
        m_y = min(weight.shape[-1], fW)
        xf = x_freq.reshape(B, n_heads, head_in, fH, fW)
        core = jnp.einsum('bhixy,hioxy->bhoxy', xf[:, :, :, :m_x, :m_y], weight[:, :, :, :m_x, :m_y])
        out_freq = jnp.zeros((B, n_heads, head_out, fH, fW), dtype=core.dtype)
        out_freq = out_freq.at[:, :, :, :m_x, :m_y].set(core)
        out_freq = out_freq.reshape(B, n_heads * head_out, fH, fW)
        x_out = jnp.fft.irfft2(out_freq, s=(H, W), axes=(-2, -1))
        return x_out + bias

    def _L1_conv_ref(x):
        import jax, jax.numpy as jnp
        import numpy as np
        M_PER_GROUP = 16
        EPS = 0.001
        b, w, h, c = x.shape
        groups = c // M_PER_GROUP
        n = b * w * h
        x_flat = jnp.transpose(x, (3, 0, 1, 2)).reshape(c, -1)
        mean = jnp.mean(x_flat, axis=1, keepdims=True)
        f = x_flat - mean
        fg = f.reshape(groups, M_PER_GROUP, -1)
        denom = jnp.float32(n) - 1.0
        cov = jnp.einsum('gmn,gkn->gmk', fg, fg) / denom
        eye = jnp.eye(M_PER_GROUP, dtype=x.dtype)
        cov = (1.0 - EPS) * cov + EPS * eye
        cov = cov / denom
        chol = jnp.linalg.cholesky(cov)
        inv_sqrt = jax.vmap(lambda L: jax.scipy.linalg.solve_triangular(L, eye, lower=True))(chol)
        f_hat = jnp.einsum('gmk,gkn->gmn', inv_sqrt, fg)
        out = f_hat.reshape(c, b, w, h)
        return jnp.transpose(out, (1, 2, 3, 0))

    def _gn(v, G=32, eps=1e-5):
        B_, C_, H_, W_ = v.shape
        g = v.reshape(B_, G, C_ // G, H_, W_)
        m = jnp.mean(g, axis=(2, 3, 4), keepdims=True)
        s = jnp.var(g, axis=(2, 3, 4), keepdims=True)
        return ((g - m) / jnp.sqrt(s + eps)).reshape(v.shape)

    def _ln_c(v, eps=1e-6):
        m = jnp.mean(v, axis=1, keepdims=True)
        s = jnp.var(v, axis=1, keepdims=True)
        return (v - m) / jnp.sqrt(s + eps)

    def _ln_t(v, eps=1e-5):
        m = jnp.mean(v, axis=-1, keepdims=True)
        s = jnp.var(v, axis=-1, keepdims=True)
        return (v - m) / jnp.sqrt(s + eps)

    def _to_tokens(v):
        B_, C_, H_, W_ = v.shape
        return v.reshape(B_, C_, H_ * W_).transpose(0, 2, 1)
    def _from_tokens(t, like):
        B_, C_, H_, W_ = like.shape
        return t.transpose(0, 2, 1).reshape(B_, C_, H_, W_)

    x = x + _L0_conv_ref(_gn(x), L0_conv_weight_re, L0_conv_weight_im, L0_conv_bias)
    x = x + _L1_conv_ref(_gn(x))
    return x


_drawn_inputs = setup_inputs


def setup_inputs(seed=0):
    import zlib

    import numpy as np

    out = dict(_drawn_inputs(seed))
    spreads = {'L0_conv_bias': (0.0, 0.1)}
    factors = {'L0_conv_weight_re': 8.0, 'L0_conv_weight_im': 8.0}
    for name, (base, spread) in spreads.items():
        noise = np.random.default_rng([zlib.crc32(name.encode()), seed]).standard_normal(out[name].shape)
        drawn = base * np.exp(spread * noise) if base else spread * noise
        out[name] = jnp.asarray(drawn.astype(out[name].dtype))
    for name, factor in factors.items():
        out[name] = (out[name] * factor).astype(out[name].dtype)
    return out
```

```python
import concourse.bass as bass
from concourse import mybir
from contextlib import ExitStack
import numpy as np

P = 128
HEADS, HC = 4, 16
PAIRS = HC // 2
H = W = 256
KX, KY = 32, 17
KH, KW = 2 * KX, 2 * KY
KG, KA = 4, 8
AREA = H * W
GROUP = 2 * AREA
M = 16
BL = 32
EPS_GN, EPS_W = 1e-5, 1e-3
RW = PAIRS * KY

COLS = dict(hc=2 * KH, ew=2 * KW, hb=2 * H, e0=W, e1=W, rot=P, fold=KW + 1, eye=P, eye32=2 * BL, dc=1, hk=1, hh=1,
            sgn=1, weigh=KW, ones=P, mean=P)


def columns():
    at, out = 0, {}
    for name, n in COLS.items():
        out[name] = (at, at + n)
        at += n
    return out, at


def tables():
    where, n = columns()
    t = np.zeros((P, n), np.float64)

    def put(name, a, rows=slice(0, P)):
        t[rows, where[name][0]:where[name][1]] = a.reshape(a.shape[0], -1)

    th = 2 * np.pi / H
    hk = np.concatenate([np.cos(th * np.outer(np.arange(KX), np.arange(H))),
                         np.sin(th * np.outer(np.arange(KX), np.arange(H)))])
    wj = np.concatenate([np.cos(th * np.outer(np.arange(KY), np.arange(W))),
                         np.sin(th * np.outer(np.arange(KY), np.arange(W)))])
    cj = np.tile(np.where(np.arange(KY) == 0, 1.0, 2.0), 2) / AREA
    cj[KY] = 0.0
    put("hc", hk.T.reshape(2, P, KH).transpose(1, 0, 2))
    put("ew", wj.T.reshape(2, P, KW).transpose(1, 0, 2))
    hb = np.zeros((2, KH, 2, H))
    hb[0, :, 0], hb[1, :, 1] = hk, hk
    put("hb", hb.reshape(P, 2 * H))
    put("e0", cj[:, None] * wj, slice(0, KW))
    put("e1", cj[:, None] * wj, slice(1, KW + 1))
    rot = np.zeros((P, P))
    for c in range(2):
        for k in range(KX):
            rot[KH * c + KX + k, KH * c + k] = -1.0
            rot[KH * c + k, KH * c + KX + k] = 1.0
    put("rot", rot)
    fold = np.zeros((P, KW + 1))
    fold[np.arange(KW + 1), np.arange(KW + 1)] = 1.0
    fold[KH + np.arange(KW + 1), np.arange(KW + 1)] = 1.0
    put("fold", fold)
    put("eye", np.eye(P))
    put("eye32", np.tile(np.eye(BL), (P // BL, 2)))
    dc = np.zeros((P, 1))
    dc[[0, KH]] = 1.0
    put("dc", dc)
    norm = np.tile(np.concatenate([[H], np.full(KX - 1, H / 2), [0], np.full(KX - 1, H / 2)]), 2)[:, None]
    put("hk", norm / (2 * H))
    put("hh", norm / 2)
    put("sgn", np.tile(np.repeat([-1.0, 1.0], HC), KG)[:, None])
    put("weigh", np.tile(2 * cj, (P, 1)))
    put("ones", np.ones((P, P)))
    put("mean", np.repeat(dc, P, 1) / GROUP)
    return t.astype(np.float32)


class Chain:

    def __init__(self, eng, sem):
        self.eng, self.sem, self.n, self.i, self.k, self.n0 = eng, sem, 0, None, 0, 0

    def value(self):
        return self.n if self.i is None else self.i * self.k + self.n

    def __call__(self, ins):
        ins.then_inc(self.sem, 1)
        self.n += 1
        self.eng.wait_ge(self.sem, self.value())

    def enter(self, i, k):
        self.i, self.k, self.n0 = i, k, self.n

    def leave(self, trips):
        assert self.n - self.n0 == self.k, (self.n, self.n0, self.k)
        self.n, self.i = self.n0 + self.k * trips, None


def whiten_kernel(nc, x, w_re, w_im, bias, table, out):
    f32 = mybir.dt.float32
    ALU, ACT, AX = mybir.AluOpType, mybir.ActivationFunctionType, mybir.AxisListType
    B = x.shape[0]
    NU, NP = B * HEADS, B * HEADS * PAIRS
    ROWS = B * HEADS * HC * H
    DENOM = ROWS - 1.0
    where, ncols = columns()
    ds = bass.ds

    x_v = x.rearrange("b c (t p) w -> p (b c) t w", p=P)
    out_v = out.rearrange("b c (t p) w -> p (b c) t w", p=P)

    xh_d = nc.dram_tensor("xh_d", (NU, P, PAIRS, W), f32, kind="Internal").ap()
    gram_d = nc.dram_tensor("gram_d", (NU, P, PAIRS * 2 * BL), f32, kind="Internal").ap()
    spec_d = nc.dram_tensor("spec_d", (HEADS, 2, PAIRS, 2, B, KX, KY), f32, kind="Internal").ap()
    conv_d = nc.dram_tensor("conv_d", (HEADS, B, 2, 2, KX, PAIRS, KY), f32, kind="Internal").ap()
    cov_d = nc.dram_tensor("cov_d", (P, 2, BL), f32, kind="Internal").ap()
    inv_d = nc.dram_tensor("inv_d", (2 * W // BL, M, M), f32, kind="Internal").ap()

    ctx = ExitStack()
    with ctx:
        def sb(name, shape):
            return ctx.enter_context(nc.sbuf_tensor(name, shape, f32))

        def sem(name):
            return ctx.enter_context(nc.semaphore(name))

        bank = [ctx.enter_context(nc.psum_tensor(f"bank{i}", [P, 512], f32)) for i in range(8)]
        tab = sb("tab", [P, ncols])
        reg1 = sb("reg1", [P, NP * KW])
        reg2 = sb("reg2", [P, max(NP * KW, 3 * 4352 + 2 * B * 136)])
        reg3 = sb("reg3", [P, max(NP * KY, 8192 + 512)])

        def T(name, rows=P):
            a, b = where[name]
            return tab[0:rows, a:b]

        def cut(reg, at, *shape):
            n = int(np.prod(shape))
            v = reg[:, at:at + n]
            if len(shape) > 1:
                names = [f"d{i}" for i in range(len(shape))]
                v = v.rearrange(f"p ({' '.join(names)}) -> p {' '.join(names)}",
                                **{k: s for k, s in zip(names[1:], shape[1:])})
            return v, at + n

        hc = T("hc").rearrange("p (t k) -> p t k", t=2)
        ew = T("ew").rearrange("p (t j) -> p t j", t=2)

        D, _ = cut(reg1, 0, NP, KW)
        C, _ = cut(reg2, 0, NP, KW)
        weights, a = cut(reg2, 0, 2, 2, HC, KA * KY)
        modes_in, a = cut(reg2, a, 2, B, KA * KY)
        modes_out, a = cut(reg2, a, 4, KA, PAIRS, KY)
        x_in, _ = cut(reg3, 0, 16, 2, W)
        PS, _ = cut(reg3, 0, NP, KY)
        CT = PS.rearrange("p (b h c) k -> p b h c k", h=HEADS, c=PAIRS)
        crs, a = cut(reg3, 0, 2, PAIRS, W + KW)
        gram_in, a = cut(reg3, a, 2, PAIRS * 2 * BL)
        gram_w, a = cut(reg3, a, PAIRS * 2 * BL)
        cr, a = cut(reg3, a, 2, PAIRS, KH)
        x_re, _ = cut(reg3, 0, 16, 2, W)

        xh = sb("xh", [P, PAIRS, W])
        xht = sb("xht", [P, 2, 2, P])
        gram = sb("gram", [P, PAIRS, 2 * BL])
        gmask = sb("gmask", [P, PAIRS, 2 * BL])
        ssq_part = sb("ssq_part", [P, NP])
        flat = lambda t: t.rearrange("p a b -> p (a b)")
        xh_f, xht_f, gmask_f = flat(xh[:, :, :]), xht[:, :, :, :].rearrange("p a b c -> p (a b c)"), flat(gmask[:, :, :])
        root_in, root_out, r0 = (xh_f[:, i * NP:i * NP + NP] for i in range(3))
        aug = xh_f[0:M, 3 * 512:4 * 512].rearrange("p (a b) -> p a b", a=M)
        step_ = xht_f[0:M, :].rearrange("p (a b) -> p a b", a=M)
        sneg = xht_f[0:1, 0:W]
        work = gmask_f[:, 0:15 * KW].rearrange("p (a b) -> p a b", b=KW)
        inv = gmask_f[0:M, 0:M * M].rearrange("p (a b) -> p a b", a=M)
        m0, ssq, tmp = sb("m0", [P, NP]), sb("ssq", [P, NP]), sb("tmp", [P, NP])
        m1, r1, r1sq = m0, ssq, ssq_part
        beta = sb("beta", [P, HEADS * PAIRS])
        qacc, a = cut(reg3, a, W + KW)
        gacc, a = cut(reg3, a, PAIRS * 2 * BL)
        R, a = cut(reg3, a, W)
        R = R[0:KW + 1]
        qt, qtp = sb("qt", [KW, KW + 1]), sb("qtp", [KW, P])
        cov, covg = sb("cov", [P, 2 * BL]), sb("covg", [P, 2 * BL])
        fac = sb("fac", [M, M])
        whit, msum, mwhit = sb("whit", [P, 2, P]), sb("msum", [P, 2, P]), sb("mwhit", [P, W])

        o_sb, a = cut(reg1, 0, 4, 4, W) if NP >= 256 else cut(sb("o_buf", [P, 4096]), 0, 4, 4, W)
        big = reg1 if NP >= 256 else sb("p2_buf", [P, 4096])
        a = a if NP >= 256 else 0
        v_sb, a = cut(big, a, 2, 512)
        xt_sb, a = cut(big, a, 2, 512)
        wr, a = cut(big, a, 2, 2, P)
        wp, a = cut(big, a, 2, 2, P)
        cs, a = cut(big, a, 4, KW)

        names = """tab_in beta_in beta_zero
            x_in0 x_in1 x_in2 x_in3 x_used0 x_used1 x_used2 x_used3 gram_mm gram_copied xh_mm xh_copied xt_mm xt_copied d_mm d_copied
            xh_out0 xh_out1 gram_out diag_done dve_chain act_chain pool_chain pe_chain
            spectra_ready stat_mm rot_mm rot_read root_wanted root_done ps_ready ps_stored
            modes_in_in0 modes_in_in1 weights_in0 weights_in1 signed mode_mm mode_act mode_dve conv_stored conv_in
            rot2_mm rot2_act c_ready m1_mm var_ready var_mm r1_ready
            crs_in0 crs_in1 gram_in0 gram_in1 cr_ready q_mm q_read gram_used
            qacc_ready qt_mm qt_ready r_mm r_ready cov_mm cov_ready cov_stored aug_in inv_ready inv_stored whit_zero whit_in
            ms_mm ms_ready mw_mm mw_ready
            cs_ready w_scaled w_ready x_re_in0 x_re_in1 x_re_in2 x_re_in3 v_mm v_copied xt2_mm xt2_copied o_mm o_ready x_re_used0 x_re_used1 x_re_used2 x_re_used3
            out_stored0 out_stored1 out_stored2 out_stored3""".split()
        S = {n: sem(n) for n in names}
        block = ctx.enter_context(nc.Block())

        @block.sync
        def _(sp):
            for name in ['gram_out', 'xh_out0', 'xh_out1']:
                sp.sem_inc(S[name], 1)
            sp.dma_start(tab[:, :], table).then_inc(S["tab_in"], 16)
            sp.wait_ge(S["beta_zero"], 1)
            for c in range(2):
                sp.dma_start(beta[KH * c:KH * c + 1, :],
                             bias.rearrange("(n c) a b -> c (n a b)", c=2)[c:c + 1, :],
                             allow_slow_non_contiguous=True).then_inc(S["beta_in"], 16)
            with sp.Fori(0, NU) as u:
                for j in range(4):
                    sp.wait_ge(S[f"x_used{j}"], u + 1)
                    sp.dma_start(x_in[:, 4 * j:4 * j + 4], x_v[:, ds(u * HC + 4 * j, 4)]).then_inc(S[f"x_in{j}"], 16)
                for j in range(2):
                    sp.wait_ge(S["xh_copied"], u * PAIRS + 4 * j + 4 + 1)
                    sp.dma_start(xh_d[ds(u, 1), :, 4 * j:4 * j + 4].rearrange("u p a w -> (u p) a w"),
                                 xh[:, 4 * j:4 * j + 4]).then_inc(S[f"xh_out{j}"], 16)
                sp.wait_ge(S["gram_copied"], u * 2 + 2 + 1)
                sp.dma_start(gram_d[ds(u, 1)].rearrange("u p a -> (u p) a"),
                             gram[:, :, :].rearrange("p a b -> p (a b)")).then_inc(S["gram_out"], 16)
            for n in ("xh_out0", "xh_out1", "gram_out"):
                sp.wait_ge(S[n], 16 * NU + 1)
            sp.wait_ge(S["ps_ready"], 1)
            with sp.Fori(0, B) as b:
                for h in range(HEADS):
                    for c in range(2):
                        for s in range(2):
                            row = KH * c + KX * s
                            sp.dma_start(spec_d[h, s, :, c, ds(b, 1)].rearrange("n b k y -> k (n b) y"),
                                         PS[row:row + KX, ds(b * (HEADS * PAIRS) + h * PAIRS, PAIRS)]
                                         ).then_inc(S["ps_stored"], 16)
            sp.wait_ge(S["ps_stored"], 16 * 16 * B)
            for h in range(HEADS + 1):
                if h < HEADS:
                    if h >= 2:
                        sp.wait_ge(S["mode_mm"], (h - 1) * 2 * KA)
                    for g in range(KG):
                        sp.dma_start(modes_in[32 * g:32 * g + 32, h % 2],
                                     spec_d[h, :, :, :, :, KA * g:KA * g + KA].rearrange(
                                         "s n c b k y -> (s n c) b (k y)")).then_inc(S[f"modes_in_in{h % 2}"], 16)
                        for s in range(2):
                            for r in range(2):
                                row = 32 * g + HC * s
                                src = (w_re, w_im)[(s + r) % 2][h, :, :, KA * g:KA * g + KA, 0:KY].rearrange(
                                    "i (n c) k y -> c i n (k y)", c=2)
                                for c in range(2):
                                    sp.dma_start(weights[row:row + HC, h % 2, r, PAIRS * c:PAIRS * c + PAIRS],
                                                 src[c]).then_inc(S[f"weights_in{h % 2}"], 16)
                if h >= 1:
                    sp.wait_ge(S["mode_act"], h * 2 * KA)
                    sp.wait_ge(S["mode_dve"], h * 2 * KA)
                    for g in range(KG):
                        for r in range(2):
                            sp.dma_start(conv_d[h - 1, :, :, r, KA * g:KA * g + KA].rearrange("b c k n y -> b c (k n y)"),
                                         modes_out[32 * g:32 * g + B, 2 * r:2 * r + 2].rearrange(
                                             "p c k n y -> p c (k n y)")).then_inc(S["conv_stored"], 16)
                    sp.wait_ge(S["conv_stored"], h * (16 * 2 * KG))
                    sp.dma_start(CT[:, :, h - 1].rearrange("p b c k -> p b (c k)"),
                                 conv_d[h - 1].rearrange("b c r k n y -> (c r k) b (n y)")).then_inc(S["conv_in"], 16)
            sp.wait_ge(S["c_ready"], 1)
            with sp.Fori(0, NU // 2) as t:
                for e in range(2):
                    sp.wait_ge(S["q_mm"], t * 2 + 1)
                    sp.wait_ge(S["gram_used"], t * 2 + 1)
                    sp.dma_start(crs[:, e, :, 0:W], xh_d[ds(t * 2 + e, 1)].rearrange("u p a w -> (u p) a w")
                                 ).then_inc(S[f"crs_in{e}"], 16)
                    sp.dma_start(gram_in[:, e], gram_d[ds(t * 2 + e, 1)].rearrange("u p a -> (u p) a")
                                 ).then_inc(S[f"gram_in{e}"], 16)
            sp.wait_ge(S["cov_ready"], 1)
            sp.dma_start(cov_d.rearrange("p a b -> p (a b)"), cov[:, :]).then_inc(S["cov_stored"], 16)
            sp.wait_ge(S["cov_stored"], 16)
            for half in range(2):
                for s in range(2):
                    for q in range(4):
                        g = 8 * half + 4 * s + q
                        row = BL * q + M * s
                        sp.dma_start(aug[g:g + 1, :, 0:M],
                                     cov_d[row:row + M, half, M * s:M * s + M].unsqueeze(0)
                                     ).then_inc(S["aug_in"], 16)
            sp.wait_ge(S["inv_ready"], 1)
            sp.dma_start(inv_d, inv[:, :, :]).then_inc(S["inv_stored"], 16)
            sp.wait_ge(S["inv_stored"], 16)
            sp.wait_ge(S["whit_zero"], 1)
            for half in range(2):
                for s in range(2):
                    for q in range(4):
                        g = 8 * half + 4 * s + q
                        row = BL * q + M * s
                        sp.dma_start(whit[row:row + M, half, row:row + M], inv_d[g]).then_inc(S["whit_in"], 16)
            sp.wait_ge(S["ms_ready"], 1)
            with sp.Fori(0, NP // 4) as t:
                for j in range(4):
                    sp.wait_ge(S[f"x_re_used{j}"], t + 1)
                    sp.dma_start(x_re[:, 2 * j:2 * j + 2], x_v[:, ds(t * 8 + 2 * j, 2)]).then_inc(S[f"x_re_in{j}"], 16)

        @block.tensor
        def _(pe):
            for name in ['o_mm', 'q_mm', 'v_mm', 'x_re_used0', 'x_re_used1', 'x_re_used2', 'x_re_used3', 'x_used0', 'x_used1', 'x_used2', 'x_used3']:
                pe.sem_inc(S[name], 1)
            mm = nc.tensor.matmul
            pe.wait_ge(S["tab_in"], 16)
            one = dict(start=True, stop=True)

            def transposes(u, q):
                if q >= 2:
                    pe.wait_ge(S["xt_copied"], u * PAIRS + q - 1 + 1)
                pe.wait_ge(S["xh_copied"], u * PAIRS + q + 1 + 1)
                for half in range(2):
                    ins = mm(bank[4 + q % 2][:, P * half:P * half + P], xh[:, q, P * half:P * half + P], T("eye"),
                             start=half == 0, stop=True, is_transpose=True, skip_group_check=True)
                ins.then_inc(S["xt_mm"], 1)

            def spectrum(u, q):
                pe.wait_ge(S["xt_copied"], u * PAIRS + q + 1 + 1)
                if q % 4 == 0:
                    pe.wait_ge(S["d_copied"], u * 2 + 1)
                for half in range(2):
                    ins = mm(bank[6 + q // 4][:, KW * (q % 4):KW * (q % 4) + KW], xht[:, q % 2, half], ew[:, half],
                             start=half == 0, stop=half == 1, skip_group_check=True)
                if q % 4 == 3:
                    ins.then_inc(S["d_mm"], 1)
                if q % 2 == 0:
                    ins.then_inc(S[f"x_used{q // 2}"], 1)

            with pe.Fori(0, NU) as u:
                for q in range(PAIRS):
                    if q % 2 == 0:
                        pe.wait_ge(S[f"x_in{q // 2}"], u * 16 + 16)
                    if q % 4 == 0:
                        pe.wait_ge(S["gram_copied"], u * 2 + 1)
                    for c in range(2):
                        for t in range(2):
                            for half in range(2):
                                for j in range(4):
                                    col = P * half + BL * j
                                    blk = x_in[:, 2 * q + c, t, col:col + BL]
                                    at = 2 * BL * (q % 4) + BL * half
                                    ins = mm(bank[q // 4][BL * j:BL * j + BL, at:at + BL], blk, blk,
                                             start=c == 0 and t == 0 and half == 0, stop=c == 1 and t == 1,
                                             skip_group_check=True)
                    if q % 4 == 3:
                        ins.then_inc(S["gram_mm"], 1)
                    pe.wait_ge(S["xh_copied"], u * PAIRS + max(q - 1, 0) + 1)
                    for t in range(2):
                        for c in range(2):
                            ins = mm(bank[2 + q % 2][KH * c:KH * c + KH, 0:W], hc[:, t], x_in[:, 2 * q + c, t],
                                     start=t == 0, stop=t == 1)
                    ins.then_inc(S["xh_mm"], 1)
                    if q >= 1:
                        transposes(u, q - 1)
                    if q >= 2:
                        spectrum(u, q - 2)
                transposes(u, PAIRS - 1)
                spectrum(u, PAIRS - 2)
                spectrum(u, PAIRS - 1)
            pe.wait_ge(S["spectra_ready"], 1)
            mm(bank[0][:, 0:NP], T("mean"), D[:, :, 0], **one).then_inc(S["stat_mm"], 1)
            mm(bank[1][:, 0:NP], T("ones"), ssq_part[:, :], **one).then_inc(S["stat_mm"], 1)
            with pe.Fori(0, NP // 32) as t:
                for e in range(2):
                    pe.wait_ge(S["rot_read"], t * 2 + 1)
                    mm(bank[2 + e][:, 0:16 * KY].rearrange("p (n y) -> p n y", y=KY), T("rot"),
                       D[:, ds(t * 32 + 16 * e, 16), KY:KW], **one).then_inc(S["rot_mm"], 1)
            for h in range(HEADS):
                pe.wait_ge(S[f"modes_in_in{h % 2}"], (h // 2 + 1) * 16 * KG)
                pe.wait_ge(S["signed"], h + 1)
                for a in range(KA):
                    for part, (y0, y1) in enumerate(((0, 9), (9, KY))):
                        n = h * 2 * KA + 2 * a + part
                        if n >= 2:
                            pe.wait_ge(S["mode_act"], n - 1)
                            pe.wait_ge(S["mode_dve"], n - 1)
                        for y in range(y0, y1):
                            for g in range(KG):
                                r = slice(32 * g, 32 * g + 32)
                                ins = mm(bank[2 * g + part][32 * g:32 * g + B, 32 * (y - y0):32 * (y - y0) + 32],
                                         modes_in[r, h % 2, :, KY * a + y],
                                         weights[r, h % 2, :, :, KY * a + y].rearrange("p r o -> p (r o)"), **one)
                        ins.then_inc(S["mode_mm"], 1)
            pe.wait_ge(S["conv_in"], 16 * HEADS)
            with pe.Fori(0, NP // 32) as t:
                for e in range(2):
                    pe.wait_ge(S["rot2_act"], t * 2 + 1)
                    mm(bank[2 + e][:, 0:16 * KY], T("rot"),
                       PS[:, ds(t * 32 + 16 * e, 16)].rearrange("p n y -> p (n y)"), **one).then_inc(S["rot2_mm"], 1)
            pe.wait_ge(S["c_ready"], 1)
            mm(bank[0][:, 0:NP], T("mean"), C[:, :, 0], **one).then_inc(S["m1_mm"], 1)
            pe.wait_ge(S["var_ready"], 1)
            mm(bank[1][:, 0:NP], T("ones"), tmp[:, :], **one).then_inc(S["var_mm"], 1)
            with pe.Fori(0, NU // 2) as t:
                for e in range(2):
                    pe.wait_ge(S[f"crs_in{e}"], t * 16 + 16)
                    pe.wait_ge(S["cr_ready"], t * 2 + e + 1)
                    pe.wait_ge(S["q_read"], t * 2 + 1)
                    for q in range(PAIRS):
                        c = q % 2
                        ins = mm(bank[2 + e][KH * c:KH * c + KH, 0:W + KW], cr[:, e, q], crs[:, e, q],
                                 start=q < 2, stop=q >= PAIRS - 2)
                    ins.then_inc(S["q_mm"], 1)
            pe.wait_ge(S["qacc_ready"], 1)
            nc.tensor.transpose(bank[0][0:KW, 0:P], qacc[:, W:W + KW], T("eye")).then_inc(S["qt_mm"], 1)
            pe.wait_ge(S["qt_ready"], 1)
            mm(bank[1][0:KW + 1, 0:W], T("fold"), qacc[:, 0:W], start=True, stop=False)
            mm(bank[1][0:KW + 1, 0:W], qt[:, :], T("e0", KW), start=False, stop=True).then_inc(S["r_mm"], 1)
            pe.wait_ge(S["r_ready"], 1)
            for half in range(2):
                for j in range(4):
                    w0 = P * half + BL * j
                    dst = bank[2][BL * j:BL * j + BL, BL * half:BL * half + BL]
                    e1 = T("e1", KW + 1)[:, w0:w0 + BL]
                    mm(dst, R[:, w0:w0 + BL], e1, start=half == 0, stop=False, skip_group_check=True)
                    mm(dst, e1, R[:, w0:w0 + BL], start=False, stop=False, skip_group_check=True)
                    ins = mm(dst, sneg[0:1, w0:w0 + BL], R[0:1, w0:w0 + BL], start=False, stop=True,
                             skip_group_check=True)
            ins.then_inc(S["cov_mm"], 1)
            for half in range(2):
                ins = mm(bank[3][:, P * half:P * half + P], R[0:1, P * half:P * half + P], T("ones", 1), start=half == 0,
                         stop=True, skip_group_check=True)
            ins.then_inc(S["ms_mm"], 1)
            pe.wait_ge(S["ms_ready"], 1)
            pe.wait_ge(S["whit_in"], 16 * 16)
            for half in range(2):
                ins = mm(bank[4][:, P * half:P * half + P], msum[:, half], whit[:, half], start=half == 0, stop=True,
                         skip_group_check=True)
            ins.then_inc(S["mw_mm"], 1)
            pe.wait_ge(S["mw_ready"], 1)
            with pe.Fori(0, NP // 4) as t:
                for q in range(4):
                    e = q % 2
                    pe.wait_ge(S["cs_ready"], t * 4 + q + 1)
                    mm(bank[e][0:KW, :], cs[:, q], T("hb"), **one).then_inc(S["v_mm"], 1)
                    pe.wait_ge(S[f"x_re_in{q}"], t * 16 + 16)
                    for half in range(2):
                        pe.wait_ge(S["xt2_copied"], t * 8 + (2 * q + half - 1 if q else 0) + 1)
                        for c in range(2):
                            for r in range(2):
                                mm(bank[2 + half][:, H * c + P * r:H * c + P * r + P],
                                   x_re[:, 2 * q + c, r, P * half:P * half + P], T("eye"), start=c == 0 and r == 0,
                                   stop=False, is_transpose=True, skip_group_check=True)
                        pe.wait_ge(S["v_copied"], t * 4 + q + 1)
                        mm(bank[2 + half][:, :], T("e0", KW)[:, P * half:P * half + P], v_sb[0:KW, e],
                           start=False, stop=True, skip_group_check=True).then_inc(S["xt2_mm"], 1)
                    pe.wait_ge(S["w_ready"], t * 4 + q + 1 + 1)
                    pe.wait_ge(S["xt2_copied"], t * 8 + 2 * q + 2 + 1)
                    for c in range(2):
                        pe.wait_ge(S["o_ready"], t * 8 + (2 * q + c - 3 if q >= 2 else 0) + 1)
                        for r in range(2):
                            for half in range(2):
                                ins = mm(bank[4 + 2 * e + c][:, W * r + P * half:W * r + P * half + P],
                                         xt_sb[:, half, H * c + P * r:H * c + P * r + P], wp[:, e, half],
                                         start=r == 0 and half == 0, stop=True, skip_group_check=True)
                                if c == 0 and r == 0 and half == 0:
                                    ins.then_inc(S[f"x_re_used{q}"], 1)
                        ins.then_inc(S["o_mm"], 1)

        def root(act, n, a):
            act.wait_ge(S["root_wanted"], n)
            nc.scalar.activation(root_out[0:a.shape[0], 0:a.shape[1]], a, ACT.Sqrt).then_inc(S["root_done"], 1)

        @block.scalar
        def _(act):
            for name in ['gram_copied', 'out_stored0', 'out_stored1', 'out_stored2', 'out_stored3', 'rot2_act', 'xh_copied', 'xt2_copied']:
                act.sem_inc(S[name], 1)
            copy = lambda o, i, **k: nc.scalar.activation(o, i, ACT.Copy, **k)
            with act.Fori(0, NU) as u:
                for q in range(PAIRS):
                    if q % 4 == 0:
                        act.wait_ge(S[f"xh_out{q // 4}"], u * 16 + 1)
                    act.wait_ge(S["xh_mm"], u * PAIRS + q + 1)
                    copy(xh[:, q], bank[2 + q % 2][:, 0:W]).then_inc(S["xh_copied"], 1)
                    if q % 4 == 3:
                        j = q // 4
                        if j == 0:
                            act.wait_ge(S["gram_out"], u * 16 + 1)
                            act.wait_ge(S["diag_done"], u + 1)
                        act.wait_ge(S["gram_mm"], u * 2 + j + 1)
                        copy(gram[:, 4 * j:4 * j + 4].rearrange("p a b -> p (a b)"),
                             bank[j][:, 0:8 * BL]).then_inc(S["gram_copied"], 1)
            root(act, 1, root_in[:, :])
            for h in range(HEADS):
                if h >= 1:
                    act.wait_ge(S["conv_stored"], h * (16 * 2 * KG))
                for a in range(KA):
                    for part, (y0, y1) in enumerate(((0, 9), (9, KY))):
                        act.wait_ge(S["mode_mm"], h * 2 * KA + 2 * a + part + 1)
                        for g in range(2):
                            ins = copy(modes_out[32 * g:32 * g + B, :, a, :, y0:y1],
                                       bank[2 * g + part][32 * g:32 * g + B, 0:32 * (y1 - y0)].rearrange(
                                           "p (y r n) -> p r n y", r=4, n=PAIRS))
                        ins.then_inc(S["mode_act"], 1)
            with act.Fori(0, NP // 32) as t:
                for e in range(2):
                    act.wait_ge(S["rot2_mm"], t * 2 + e + 1)
                    copy(C[:, ds(t * 32 + 16 * e, 16), KY:KW],
                         bank[2 + e][:, 0:16 * KY].rearrange("p (n y) -> p n y", y=KY),
                         scale=-1.0).then_inc(S["rot2_act"], 1)
            root(act, 2, root_in[:, :])
            act.wait_ge(S["qt_mm"], 1)
            copy(qtp[:, :], bank[0][0:KW, 0:P]).then_inc(S["act_chain"], 1)
            act.wait_ge(S["ms_mm"], 1)
            copy(msum[:, :, :].rearrange("p a b -> p (a b)"), bank[3][:, 0:W]).then_inc(S["ms_ready"], 1)
            root(act, 3, root_in[0:M, 0:M])
            act.wait_ge(S["mw_mm"], 1)
            copy(mwhit[:, :], bank[4][:, 0:W], scale=1.0 / ROWS).then_inc(S["mw_ready"], 1)
            with act.Fori(0, NP // 4) as t:
                for q in range(4):
                    e = q % 2
                    act.wait_ge(S["w_ready"], t * 4 + max(q - 1, 0) + 1)
                    copy(wr[:, e].rearrange("p a b -> p (a b)"), whit[:, :, :].rearrange("p a b -> p (a b)"),
                         scale=r1[:, ds(t * 4 + q, 1)]).then_inc(S["w_scaled"], 1)
                    act.wait_ge(S["v_mm"], t * 4 + q + 1 + 1)
                    copy(v_sb[0:KW, e], bank[e][0:KW, :]).then_inc(S["v_copied"], 1)
                    act.wait_ge(S["xt2_mm"], t * 8 + 2 * q + 1)
                    act.wait_ge(S["o_mm"], t * 8 + 2 * q + 1)
                    copy(xt_sb[:, 0], bank[2][:, :]).then_inc(S["xt2_copied"], 1)
                    act.wait_ge(S["xt2_mm"], t * 8 + 2 * q + 2)
                    copy(xt_sb[:, 1], bank[3][:, :]).then_inc(S["xt2_copied"], 1)
                    act.wait_ge(S["o_ready"], t * 8 + 2 * q + 2 + 1)
                    act.dma_start(out_v[:, ds(t * 8 + 2 * q, 2)],
                                  o_sb[:, q].rearrange("p (c r) w -> p c r w", c=2)).then_inc(S[f"out_stored{q}"], 16)
            for q in range(4):
                act.wait_ge(S[f"out_stored{q}"], 16 * (NP // 4) + 1)

        @block.gpsimd
        def _(pool):
            for name in ['gram_used', 'w_ready']:
                pool.sem_inc(S[name], 1)
            pch = Chain(pool, S["pool_chain"])
            pch(nc.gpsimd.memset(beta[:, :], 0.0))
            pool.sem_inc(S["beta_zero"], 1)
            pch(nc.gpsimd.memset(whit[:, :, :], 0.0))
            pool.sem_inc(S["whit_zero"], 1)
            pool.wait_ge(S["r1_ready"], 1)
            pch(nc.gpsimd.memset(gacc, 0.0))
            pch.enter(None, 0)
            with pool.Fori(0, NU // 2) as t:
                pch.enter(t, 4)
                for e in range(2):
                    pool.wait_ge(S[f"gram_in{e}"], t * 16 + 16)
                    g3 = lambda a: a.rearrange("p (n b) -> p n b", b=2 * BL)
                    pch(nc.gpsimd.tensor_tensor(
                        out=g3(gram_w), in0=g3(gram_in[:, e]),
                        in1=r1sq[:, ds((t * 2 + e) * PAIRS, PAIRS)].unsqueeze(2).to_broadcast([P, PAIRS, 2 * BL]),
                        op=ALU.mult))
                    pch(nc.gpsimd.tensor_tensor(out=gacc, in0=gacc, in1=gram_w, op=ALU.add))
                    pool.sem_inc(S["gram_used"], 1)
            pch.leave(NU // 2)
            pool.wait_ge(S["mw_ready"], 1)
            with pool.Fori(0, NP // 4) as t:
                for q in range(4):
                    e = q % 2
                    pool.wait_ge(S["v_mm"], t * 4 + 1)
                    nc.gpsimd.tensor_copy(cs[:, q], C[:, ds(t * 4 + q, 1)].rearrange("p a b -> p (a b)")
                                          ).then_inc(S["cs_ready"], 1)
                    pool.wait_ge(S["w_scaled"], t * 4 + q + 1)
                    pool.wait_ge(S["o_mm"], t * 8 + max(2 * q - 2, 0) + 1)
                    nc.gpsimd.tensor_tensor(out=wp[:, e], in0=wr[:, e],
                                            in1=T("eye").unsqueeze(1).to_broadcast([P, 2, P]),
                                            op=ALU.add).then_inc(S["w_ready"], 1)

        @block.vector
        def _(dve):
            for name in ['d_copied', 'diag_done', 'o_ready', 'q_read', 'rot_read', 'xt_copied']:
                dve.sem_inc(S[name], 1)
            v = nc.vector
            ch = Chain(dve, S["dve_chain"])

            def inverse_root(n, r, a):
                dve.sem_inc(S["root_wanted"], 1)
                dve.wait_ge(S["root_done"], n)
                t = root_out[0:a.shape[0], 0:a.shape[1]]
                ch(v.reciprocal(r, t))
                ch(v.tensor_tensor(out=t, in0=r, in1=r, op=ALU.mult))
                ch(v.tensor_tensor(out=t, in0=t, in1=a, op=ALU.mult))
                ch(v.tensor_scalar(t, t, -0.5, 1.5, ALU.mult, ALU.add))
                ch(v.tensor_tensor(out=r, in0=r, in1=t, op=ALU.mult))

            dve.wait_ge(S["tab_in"], 16)
            with dve.Fori(0, NU) as u:
                ch.enter(u, 2)
                for q in range(PAIRS):
                    dve.wait_ge(S["xt_mm"], u * PAIRS + q + 1)
                    if q % 4 >= 2 or q < 2:
                        pass
                    v.tensor_copy(xht[:, q % 2].rearrange("p a b -> p (a b)"),
                                  bank[4 + q % 2][:, 0:W]).then_inc(S["xt_copied"], 1)
                    if q == 5:
                        dve.wait_ge(S["d_mm"], u * 2 + 1)
                        v.tensor_copy(D[:, ds(u * PAIRS, 4)].rearrange("p a b -> p (a b)"),
                                      bank[6][:, 0:4 * KW]).then_inc(S["d_copied"], 1)
                dve.wait_ge(S["d_mm"], u * 2 + 2)
                v.tensor_copy(D[:, ds(u * PAIRS + 4, 4)].rearrange("p a b -> p (a b)"),
                              bank[7][:, 0:4 * KW]).then_inc(S["d_copied"], 1)
                dve.wait_ge(S["gram_copied"], u * 2 + 2 + 1)
                ch(v.tensor_tensor(out=gmask[:, :, :], in0=gram[:, :, :],
                                   in1=T("eye32").unsqueeze(1).to_broadcast([P, PAIRS, 2 * BL]), op=ALU.mult))
                ch(v.tensor_reduce(out=ssq_part[:, ds(u * PAIRS, PAIRS)], in_=gmask[:, :, :], axis=AX.X, op=ALU.add))
                dve.sem_inc(S["diag_done"], 1)
            ch.leave(NU)
            dve.wait_ge(S["d_copied"], 2 * NU + 1)
            dve.sem_inc(S["spectra_ready"], 1)
            for n in ("xh_out0", "xh_out1", "gram_out"):
                dve.wait_ge(S[n], 16 * NU + 1)
            dve.wait_ge(S["stat_mm"], 2)
            ch(v.tensor_copy(m0[:, :], bank[0][:, 0:NP]))
            ch(v.tensor_copy(ssq[:, :], bank[1][:, 0:NP]))
            ch(v.tensor_tensor(out=tmp[:, :], in0=m0[:, :], in1=m0[:, :], op=ALU.mult))
            ch(v.scalar_tensor_tensor(out=r0[:, :], in0=ssq[:, :], scalar=1.0 / GROUP, in1=tmp[:, :],
                                      op0=ALU.mult, op1=ALU.subtract))
            ch(v.tensor_scalar(root_in[:, :], r0[:, :], EPS_GN, None, ALU.add))
            inverse_root(1, r0[:, :], root_in[:, :])
            with dve.Fori(0, NP // 32) as t:
                for e in range(2):
                    dve.wait_ge(S["rot_mm"], t * 2 + e + 1)
                    n = ds(t * 32 + 16 * e, 16)
                    v.tensor_tensor(out=PS[:, n], in0=bank[2 + e][:, 0:16 * KY].rearrange("p (n y) -> p n y", y=KY),
                                    in1=D[:, n, 0:KY], op=ALU.add).then_inc(S["rot_read"], 1)
            dve.wait_ge(S["rot_read"], NP // 16 + 1)
            ch(v.tensor_scalar(tmp[:, :], m0[:, :], T("dc"), -float(AREA), ALU.mult, ALU.mult))
            ch(v.tensor_tensor(out=PS[:, :, 0], in0=PS[:, :, 0], in1=tmp[:, :], op=ALU.add))
            ch(v.tensor_tensor(out=PS[:, :, :], in0=PS[:, :, :],
                               in1=r0[:, :].unsqueeze(2).to_broadcast([P, NP, KY]), op=ALU.mult))
            dve.sem_inc(S["ps_ready"], 1)

            def sign(h):
                dve.wait_ge(S[f"weights_in{h % 2}"], (h // 2 + 1) * (16 * 32))
                ch(v.tensor_scalar(weights[:, h % 2, 1], weights[:, h % 2, 1], T("sgn"), None, ALU.mult))
                dve.sem_inc(S["signed"], 1)

            sign(0)
            for h in range(HEADS):
                if h >= 1:
                    dve.wait_ge(S["conv_stored"], h * (16 * 2 * KG))
                for a in range(KA):
                    if a == 4 and h + 1 < HEADS:
                        sign(h + 1)
                    for part, (y0, y1) in enumerate(((0, 9), (9, KY))):
                        dve.wait_ge(S["mode_mm"], h * 2 * KA + 2 * a + part + 1)
                        for g in range(2, 4):
                            ins = v.tensor_copy(modes_out[32 * g:32 * g + B, :, a, :, y0:y1],
                                                bank[2 * g + part][32 * g:32 * g + B, 0:32 * (y1 - y0)].rearrange(
                                                    "p (y r n) -> p r n y", r=4, n=PAIRS))
                        ins.then_inc(S["mode_dve"], 1)
            dve.wait_ge(S["conv_in"], 16 * HEADS)
            dve.wait_ge(S["conv_stored"], HEADS * 16 * 2 * KG)
            ch(v.tensor_copy(C[:, :, 0:KY], PS[:, :, :]))
            dve.wait_ge(S["beta_in"], 32)
            b0 = C[:, :, 0].rearrange("p (b n) -> p b n", n=HEADS * PAIRS)
            ch(v.scalar_tensor_tensor(out=b0, in0=beta[:, :].unsqueeze(1).to_broadcast([P, B, HEADS * PAIRS]),
                                      scalar=float(AREA), in1=b0, op0=ALU.mult, op1=ALU.add))
            dve.wait_ge(S["rot2_act"], NP // 16 + 1)
            dve.sem_inc(S["c_ready"], 1)
            dve.wait_ge(S["m1_mm"], 1)
            ch(v.tensor_tensor(out=m1[:, :], in0=bank[0][:, 0:NP], in1=m0[:, :], op=ALU.add))
            ch(v.tensor_scalar(tmp[:, :], m1[:, :], T("dc"), -float(AREA), ALU.mult, ALU.mult))
            ch(v.tensor_tensor(out=C[:, :, 0], in0=C[:, :, 0], in1=tmp[:, :], op=ALU.add))
            for n in range(0, NP, 15):
                s = slice(n, min(n + 15, NP))
                k = s.stop - s.start
                wk = work[:, 0:k]
                ch(v.scalar_tensor_tensor(out=wk, in0=C[:, s], scalar=T("hk"), in1=D[:, s], op0=ALU.mult, op1=ALU.add))
                ch(v.tensor_tensor(out=wk, in0=wk, in1=C[:, s], op=ALU.mult))
                ch(v.tensor_tensor(out=wk, in0=wk, in1=T("weigh").unsqueeze(1).to_broadcast([P, k, KW]), op=ALU.mult))
                ch(v.tensor_reduce(out=tmp[:, s], in_=wk, axis=AX.X, op=ALU.add))
            dve.sem_inc(S["var_ready"], 1)
            dve.wait_ge(S["var_mm"], 1)
            ch(v.tensor_tensor(out=r1[:, :], in0=bank[1][:, 0:NP], in1=ssq[:, :], op=ALU.add))
            ch(v.tensor_scalar(root_in[:, :], r1[:, :], 1.0 / GROUP, EPS_GN, ALU.mult, ALU.add))
            inverse_root(2, r1[:, :], root_in[:, :])
            ch(v.tensor_tensor(out=r1sq[:, :], in0=r1[:, :], in1=r1[:, :], op=ALU.mult))
            ch(v.memset(qacc, 0.0))
            ch(v.memset(cr.rearrange("p a b c -> p (a b c)"), 0.0))
            dve.sem_inc(S["r1_ready"], 1)
            with dve.Fori(0, NU // 2) as t:
                ch.enter(t, 8)
                for e in range(2):
                    n = ds((t * 2 + e) * PAIRS, PAIRS)
                    dve.wait_ge(S["q_mm"], t * 2 + 1)
                    ch(v.tensor_scalar(crs[:, e, :, W:W + KW], C[:, n], T("hh"), None, ALU.mult))
                    ch(v.tensor_tensor(out=cr[:, e, :, 1:KW + 1], in0=C[:, n],
                                       in1=r1sq[:, n].unsqueeze(2).to_broadcast([P, PAIRS, KW]), op=ALU.mult))
                    ch(v.tensor_scalar(cr[:, e, :, 0], r1[:, n], T("dc"), None, ALU.mult))
                    dve.sem_inc(S["cr_ready"], 1)
                for e in range(2):
                    dve.wait_ge(S["q_mm"], t * 2 + e + 1 + 1)
                    ch(v.tensor_tensor(out=qacc, in0=bank[2 + e][:, 0:W + KW], in1=qacc, op=ALU.add))
                    dve.sem_inc(S["q_read"], 1)
            ch.leave(NU // 2)
            dve.sem_inc(S["qacc_ready"], 1)
            dve.wait_ge(S["act_chain"], 1)
            ch(v.tensor_tensor(out=qt[:, :], in0=qtp[:, 0:KW + 1], in1=qtp[:, KH:KH + KW + 1], op=ALU.add))
            ch(v.tensor_scalar(qt[:, 0:1], qt[:, 0:1], 2.0, None, ALU.mult))
            dve.sem_inc(S["qt_ready"], 1)
            dve.wait_ge(S["r_mm"], 1)
            ch(v.tensor_copy(R[:, :], bank[1][0:KW + 1, 0:W]))
            ch(v.tensor_scalar(sneg[:, :], R[0:1, :], -1.0 / ROWS, None, ALU.mult))
            dve.sem_inc(S["r_ready"], 1)
            dve.wait_ge(S["gram_used"], NU + 1)
            ch(v.tensor_reduce(out=covg[:, :], in_=gacc.rearrange("p (n b) -> p b n", b=2 * BL), axis=AX.X,
                               op=ALU.add))
            dve.wait_ge(S["cov_mm"], 1)
            ch(v.tensor_tensor(out=cov[:, :], in0=bank[2][:, 0:2 * BL], in1=covg[:, :], op=ALU.add))
            ch(v.tensor_scalar(cov[:, :], cov[:, :], (1.0 - EPS_W) / DENOM / DENOM, None, ALU.mult))
            ch(v.scalar_tensor_tensor(out=cov[:, :], in0=T("eye32"), scalar=EPS_W / DENOM, in1=cov[:, :],
                                      op0=ALU.mult, op1=ALU.add))
            dve.sem_inc(S["cov_ready"], 1)
            ch(v.memset(aug[:, :, M:2 * M], 0.0))
            diag = aug[:, :, :].rearrange("p a b -> p (a b)")
            ch(v.memset(diag[:, M:M + (2 * M + 1) * (M - 1) + 1:2 * M + 1], 1.0))
            dve.wait_ge(S["aug_in"], 16 * 16)
            for j in range(M - 1):
                n = M - 1 - j
                ch(v.reciprocal(fac[:, 0:1], aug[:, j, j:j + 1]))
                ch(v.tensor_scalar(fac[:, 1:1 + n], aug[:, j + 1:M, j], fac[:, 0:1], None, ALU.mult))
                ch(v.tensor_tensor(out=step_[:, 0:n], in0=aug[:, j, :].unsqueeze(1).to_broadcast([M, n, 2 * M]),
                                   in1=fac[:, 1:1 + n].unsqueeze(2).to_broadcast([M, n, 2 * M]), op=ALU.mult))
                ch(v.tensor_tensor(out=aug[:, j + 1:M], in0=aug[:, j + 1:M], in1=step_[:, 0:n], op=ALU.subtract))
            ch(v.tensor_copy(root_in[0:M, 0:M], diag[:, 0:(2 * M + 1) * (M - 1) + 1:2 * M + 1]))
            inverse_root(3, fac[:, :], root_in[0:M, 0:M])
            ch(v.tensor_tensor(out=inv[:, :, :], in0=aug[:, :, M:2 * M].rearrange("p m k -> p k m"),
                               in1=fac[:, :].unsqueeze(1).to_broadcast([M, M, M]), op=ALU.mult))
            dve.sem_inc(S["inv_ready"], 1)
            dve.wait_ge(S["mw_ready"], 1)
            with dve.Fori(0, NP // 4) as t:
                for q in range(4):
                    e = q % 2
                    dve.wait_ge(S[f"out_stored{q}"], t * 16 + 1)
                    for c in range(2):
                        dve.wait_ge(S["o_mm"], t * 8 + 2 * q + c + 1 + 1)
                        v.scalar_tensor_tensor(
                            out=o_sb[:, q, 2 * c:2 * c + 2],
                            in0=bank[4 + 2 * e + c][:, :].rearrange("p (r w) -> p r w", r=2),
                            scalar=m1[:, ds(t * 4 + q, 1)],
                            in1=mwhit[:, :].unsqueeze(1).to_broadcast([P, 2, W]),
                            op0=ALU.add, op1=ALU.subtract).then_inc(S["o_ready"], 1)


_INS = ["x", "L0_conv_weight_re", "L0_conv_weight_im", "L0_conv_bias"]


def kernel(**inputs):
    import concourse.bacc as _bacc
    from concourse.bass_utils import run_bass_kernel_spmd as _run

    nc = _bacc.Bacc("TRN2", target_bir_lowering=False, num_devices=1)
    arrays, args = {}, []
    for name in _INS:
        a = np.ascontiguousarray(inputs[name])
        arrays[f"in_{name}_dram"] = a
        args.append(nc.dram_tensor(f"in_{name}_dram", a.shape, mybir.dt.from_np(a.dtype), kind="ExternalInput").ap())
    table = tables()
    arrays["table_dram"] = table
    args.append(nc.dram_tensor("table_dram", table.shape, mybir.dt.float32, kind="ExternalInput").ap())
    shape = tuple(inputs["x"].shape)
    args.append(nc.dram_tensor("out_0_dram", shape, mybir.dt.float32, kind="ExternalOutput").ap())
    whiten_kernel(nc, *args)
    r = _run(nc, [arrays], core_ids=[0])
    return r.results[0]["out_0_dram"]
```

```python
import concourse.bass as bass
from concourse import mybir
from contextlib import ExitStack
import numpy as np

P = 128
HEADS, HC = 4, 16
PAIRS = HC // 2
H = W = 256
KX, KY = 32, 17
KH, KW = 2 * KX, 2 * KY
KG, KA = 4, 8
AREA = H * W
GROUP = 2 * AREA
M = 16
BL = 32
EPS_GN, EPS_W = 1e-5, 1e-3
RW = PAIRS * KY

COLS = dict(hc=2 * KH, ew=2 * KW, hb=2 * H, e0=W, e1=W, rot=P, fold=KW + 1, eye=P, eye32=2 * BL, dc=1, hk=1, hh=1,
            sgn=1, dcrow=1, pick=PAIRS, weigh=KW, ones=P, mean=P)


def columns():
    at, out = 0, {}
    for name, n in COLS.items():
        out[name] = (at, at + n)
        at += n
    return out, at


def tables():
    where, n = columns()
    t = np.zeros((P, n), np.float64)

    def put(name, a, rows=slice(0, P)):
        t[rows, where[name][0]:where[name][1]] = a.reshape(a.shape[0], -1)

    th = 2 * np.pi / H
    hk = np.concatenate([np.cos(th * np.outer(np.arange(KX), np.arange(H))),
                         np.sin(th * np.outer(np.arange(KX), np.arange(H)))])
    wj = np.concatenate([np.cos(th * np.outer(np.arange(KY), np.arange(W))),
                         np.sin(th * np.outer(np.arange(KY), np.arange(W)))])
    cj = np.tile(np.where(np.arange(KY) == 0, 1.0, 2.0), 2) / AREA
    cj[KY] = 0.0
    put("hc", hk.T.reshape(2, P, KH).transpose(1, 0, 2))
    put("ew", wj.T.reshape(2, P, KW).transpose(1, 0, 2))
    hb = np.zeros((2, KH, 2, H))
    hb[0, :, 0], hb[1, :, 1] = hk, hk
    put("hb", hb.reshape(P, 2 * H))
    put("e0", cj[:, None] * wj, slice(0, KW))
    put("e1", cj[:, None] * wj, slice(1, KW + 1))
    rot = np.zeros((P, P))
    for c in range(2):
        for k in range(KX):
            rot[KH * c + KX + k, KH * c + k] = -1.0
            rot[KH * c + k, KH * c + KX + k] = 1.0
    put("rot", rot)
    fold = np.zeros((P, KW + 1))
    fold[np.arange(KW + 1), np.arange(KW + 1)] = 1.0
    fold[KH + np.arange(KW + 1), np.arange(KW + 1)] = 1.0
    put("fold", fold)
    put("eye", np.eye(P))
    put("eye32", np.tile(np.eye(BL), (P // BL, 2)))
    dc = np.zeros((P, 1))
    dc[[0, KH]] = 1.0
    put("dc", dc)
    norm = np.tile(np.concatenate([[H], np.full(KX - 1, H / 2), [0], np.full(KX - 1, H / 2)]), 2)[:, None]
    put("hk", norm / (2 * H))
    put("hh", norm / 2)
    put("sgn", np.tile(np.repeat([-1.0, 1.0], HC), KG)[:, None])
    rows = np.arange(P)
    put("dcrow", np.where(rows < HC, -float(AREA), 0.0)[:, None])
    put("pick", (rows[:, None] // 2 % PAIRS == np.arange(PAIRS)).astype(float))
    put("weigh", np.tile(2 * cj, (P, 1)))
    put("ones", np.ones((P, P)))
    put("mean", np.repeat(dc, P, 1) / GROUP)
    return t.astype(np.float32)


class Chain:

    def __init__(self, eng, sem):
        self.eng, self.sem, self.n, self.i, self.k, self.n0 = eng, sem, 0, None, 0, 0

    def value(self):
        return self.n if self.i is None else self.i * self.k + self.n

    def __call__(self, ins):
        ins.then_inc(self.sem, 1)
        self.n += 1
        self.eng.wait_ge(self.sem, self.value())

    def enter(self, i, k):
        self.i, self.k, self.n0 = i, k, self.n

    def leave(self, trips):
        assert self.n - self.n0 == self.k, (self.n, self.n0, self.k)
        self.n, self.i = self.n0 + self.k * trips, None


def whiten_kernel(nc, x, w_re, w_im, bias, table, out):
    f32 = mybir.dt.float32
    ALU, ACT, AX = mybir.AluOpType, mybir.ActivationFunctionType, mybir.AxisListType
    B = x.shape[0]
    NU, NP = B * HEADS, B * HEADS * PAIRS
    ROWS = B * HEADS * HC * H
    DENOM = ROWS - 1.0
    where, ncols = columns()
    ds = bass.ds

    x_v = x.rearrange("b c (t p) w -> p (b c) t w", p=P)
    out_v = out.rearrange("b c (t p) w -> p (b c) t w", p=P)

    xh_d = nc.dram_tensor("xh_d", (NU, P, PAIRS, W), f32, kind="Internal").ap()
    gram_d = nc.dram_tensor("gram_d", (NU, P, PAIRS * 2 * BL), f32, kind="Internal").ap()
    spec_d = nc.dram_tensor("spec_d", (2, PAIRS, 2, NU, KX, KY), f32, kind="Internal").ap()
    conv_d = nc.dram_tensor("conv_d", (HEADS, B, 2, 2, KX, PAIRS, KY), f32, kind="Internal").ap()
    cov_d = nc.dram_tensor("cov_d", (P, 2, BL), f32, kind="Internal").ap()
    inv_d = nc.dram_tensor("inv_d", (2 * W // BL, M, M), f32, kind="Internal").ap()

    ctx = ExitStack()
    with ctx:
        def sb(name, shape):
            return ctx.enter_context(nc.sbuf_tensor(name, shape, f32))

        def sem(name):
            return ctx.enter_context(nc.semaphore(name))

        bank = [ctx.enter_context(nc.psum_tensor(f"bank{i}", [P, 512], f32)) for i in range(8)]
        tab = sb("tab", [P, ncols])
        reg1 = sb("reg1", [P, NP * KW])
        reg2 = sb("reg2", [P, max(NP * KW, 3 * 4352 + 2 * B * 136)])
        reg3 = sb("reg3", [P, max(NP * KY, 8192 + 512)])

        def T(name, rows=P):
            a, b = where[name]
            return tab[0:rows, a:b]

        def cut(reg, at, *shape):
            n = int(np.prod(shape))
            v = reg[:, at:at + n]
            if len(shape) > 1:
                names = [f"d{i}" for i in range(len(shape))]
                v = v.rearrange(f"p ({' '.join(names)}) -> p {' '.join(names)}",
                                **{k: s for k, s in zip(names[1:], shape[1:])})
            return v, at + n

        hc = T("hc").rearrange("p (t k) -> p t k", t=2)
        ew = T("ew").rearrange("p (t j) -> p t j", t=2)

        D, _ = cut(reg1, 0, NP, KW)
        C, _ = cut(reg2, 0, NP, KW)
        weights, a = cut(reg2, 0, 2, 2, HC, KA * KY)
        modes_in, a = cut(reg2, a, 2, B, KA * KY)
        modes_out, a = cut(reg2, a, 4, KA, PAIRS, KY)
        x_in, _ = cut(reg3, 0, 16, 2, W)
        CTf, _ = cut(reg3, 0, NP, KY)
        CT = CTf.rearrange("p (b h c) k -> p b h c k", h=HEADS, c=PAIRS)
        crs, a = cut(reg3, 0, 2, PAIRS, W + KW)
        gram_in, a = cut(reg3, a, 2, PAIRS * 2 * BL)
        gram_w, a = cut(reg3, a, PAIRS * 2 * BL)
        cr, a = cut(reg3, a, 2, PAIRS, KH)
        x_re, _ = cut(reg3, 0, 16, 2, W)

        xh = sb("xh", [P, PAIRS, W])
        psu = sb("psu", [P, PAIRS, KY])
        xht = sb("xht", [P, 2, 2, P])
        gram = sb("gram", [P, PAIRS, 2 * BL])
        gmask = sb("gmask", [P, PAIRS, 2 * BL])
        ssq_part = sb("ssq_part", [P, NP])
        flat = lambda t: t.rearrange("p a b -> p (a b)")
        xh_f, xht_f, gmask_f = flat(xh[:, :, :]), xht[:, :, :, :].rearrange("p a b c -> p (a b c)"), flat(gmask[:, :, :])
        root_in, root_out, r0 = (xh_f[:, i * NP:i * NP + NP] for i in range(3))
        aug = xh_f[0:M, 3 * 512:4 * 512].rearrange("p (a b) -> p a b", a=M)
        step_ = xht_f[0:M, :].rearrange("p (a b) -> p a b", a=M)
        pick = gmask_f[:, 0:NP].rearrange("p (u n) -> p u n", n=PAIRS)
        m0_row, r0_row = xht_f[:, 0:NU], xht_f[:, NU:2 * NU]
        sneg = xht_f[0:1, 0:W]
        work = gmask_f[:, 0:15 * KW].rearrange("p (a b) -> p a b", b=KW)
        inv = gmask_f[0:M, 0:M * M].rearrange("p (a b) -> p a b", a=M)
        m0, ssq, tmp = sb("m0", [P, NP]), sb("ssq", [P, NP]), sb("tmp", [P, NP])
        m1, r1, r1sq = m0, ssq, ssq_part
        beta = sb("beta", [P, HEADS * PAIRS])
        qacc, a = cut(reg3, a, W + KW)
        gacc, a = cut(reg3, a, PAIRS * 2 * BL)
        R, a = cut(reg3, a, W)
        R = R[0:KW + 1]
        qt, qtp = sb("qt", [KW, KW + 1]), sb("qtp", [KW, P])
        cov, covg = sb("cov", [P, 2 * BL]), sb("covg", [P, 2 * BL])
        fac = sb("fac", [M, M])
        whit, msum, mwhit = sb("whit", [P, 2, P]), sb("msum", [P, 2, P]), sb("mwhit", [P, W])

        o_sb, a = cut(reg1, 0, 4, 4, W) if NP >= 256 else cut(sb("o_buf", [P, 4096]), 0, 4, 4, W)
        big = reg1 if NP >= 256 else sb("p2_buf", [P, 5120])
        a = a if NP >= 256 else 0
        v_sb, a = cut(big, a, 2, 512)
        xt_sb, a = cut(big, a, 2, 2, 512)
        wr, a = cut(big, a, 2, 2, P)
        wp, a = cut(big, a, 2, 2, P)
        cs, a = cut(big, a, 4, KW)

        names = """tab_in beta_in beta_zero
            x_in0 x_in1 x_in2 x_in3 x_used0 x_used1 x_used2 x_used3 gram_mm gram_copied xh_mm xh_copied xt_mm xt_copied d_mm d_copied
            xh_out0 xh_out1 gram_out diag_done dve_chain act_chain pool_chain pe_chain
            spectra_ready stat_mm rot_mm rot_read root_wanted root_done ps_ready ps_stored
            modes_in_in0 modes_in_in1 weights_in0 weights_in1 signed mode_mm mode_act mode_dve conv_stored conv_in
            rot2_mm rot2_act c_ready m1_mm var_ready var_mm r1_ready
            crs_in0 crs_in1 gram_in0 gram_in1 cr_ready q_mm q_read gram_used
            qacc_ready qt_mm qt_ready r_mm r_ready cov_mm cov_ready cov_stored aug_in inv_ready inv_stored whit_zero whit_in
            ms_mm ms_ready mw_mm mw_ready
            cs_ready w_scaled w_ready x_re_in0 x_re_in1 x_re_in2 x_re_in3 v_mm v_copied xt2_mm xt2_copied o_mm o_ready x_re_used0 x_re_used1 x_re_used2 x_re_used3
            out_stored0 out_stored1 out_stored2 out_stored3""".split()
        HEAD = dict(sync=dict(ps_stored=1),
                    tensor=dict(x_used0=1, x_used1=1, x_used2=1, x_used3=1, q_mm=2, v_mm=4, xt2_mm=4, o_mm=4,
                                x_re_used0=1, x_re_used1=1, x_re_used2=1, x_re_used3=1),
                    scalar=dict(xh_copied=2, gram_copied=2, rot2_act=1, xt2_copied=2, v_copied=2, xh_out0=1,
                                xh_out1=1, gram_out=1, out_stored0=1, out_stored1=1, out_stored2=1, out_stored3=1),
                    vector=dict(xt_copied=2, d_copied=1, diag_done=1, rot_read=1, q_read=2, o_ready=4),
                    gpsimd=dict(gram_used=2, w_ready=2))
        START = {name: k for starts in HEAD.values() for name, k in starts.items()}
        S = {n: sem(n) for n in names}

        def nth(name, n):
            return S[name], START.get(name, 0) + n

        def head_start(eng, which):
            for name, k in HEAD[which].items():
                eng.sem_inc(S[name], k)

        block = ctx.enter_context(nc.Block())

        @block.sync
        def _(sp):
            head_start(sp, "sync")
            sp.dma_start(tab[:, :], table).then_inc(S["tab_in"], 16)
            sp.wait_ge(*nth("beta_zero", 1))
            for c in range(2):
                sp.dma_start(beta[KH * c:KH * c + 1, :],
                             bias.rearrange("(n c) a b -> c (n a b)", c=2)[c:c + 1, :],
                             allow_slow_non_contiguous=True).then_inc(S["beta_in"], 16)
            def loads(u):
                for j in range(4):
                    sp.wait_ge(*nth(f"x_used{j}", u))
                    sp.dma_start(x_in[:, 4 * j:4 * j + 4], x_v[:, ds(u * HC + 4 * j, 4)]).then_inc(S[f"x_in{j}"], 16)

            def spectra_out(u):
                sp.wait_ge(*nth("rot_read", u + 1))
                for c in range(2):
                    for s in range(2):
                        row = KH * c + KX * s
                        sp.dma_start(spec_d[s, :, c, ds(u, 1)].rearrange("n u k y -> k (n u) y"),
                                     psu[row:row + KX]).then_inc(S["ps_stored"], 16)

            loads(0)
            with sp.Fori(1, NU) as u:
                loads(u)
                spectra_out(u - 1)
            spectra_out(NU - 1)
            for n in ("xh_out0", "xh_out1", "gram_out"):
                sp.wait_ge(*nth(n, 16 * NU))
            sp.wait_ge(*nth("ps_stored", 16 * 4 * NU))
            for h in range(HEADS + 1):
                if h < HEADS:
                    if h >= 2:
                        sp.wait_ge(*nth("mode_mm", (h - 1) * 2 * KA))
                    for g in range(KG):
                        sp.dma_start(modes_in[32 * g:32 * g + 32, h % 2],
                                     spec_d[:, :, :, h:NU:HEADS, KA * g:KA * g + KA].rearrange(
                                         "s n c b k y -> (s n c) b (k y)")).then_inc(S[f"modes_in_in{h % 2}"], 16)
                        for s in range(2):
                            for r in range(2):
                                row = 32 * g + HC * s
                                src = (w_re, w_im)[(s + r) % 2][h, :, :, KA * g:KA * g + KA, 0:KY].rearrange(
                                    "i (n c) k y -> c i n (k y)", c=2)
                                for c in range(2):
                                    sp.dma_start(weights[row:row + HC, h % 2, r, PAIRS * c:PAIRS * c + PAIRS],
                                                 src[c]).then_inc(S[f"weights_in{h % 2}"], 16)
                if h >= 1:
                    sp.wait_ge(*nth("mode_act", h * 2 * KA))
                    sp.wait_ge(*nth("mode_dve", h * 2 * KA))
                    for g in range(KG):
                        for r in range(2):
                            sp.dma_start(conv_d[h - 1, :, :, r, KA * g:KA * g + KA].rearrange("b c k n y -> b c (k n y)"),
                                         modes_out[32 * g:32 * g + B, 2 * r:2 * r + 2].rearrange(
                                             "p c k n y -> p c (k n y)")).then_inc(S["conv_stored"], 16)
                    sp.wait_ge(*nth("conv_stored", h * (16 * 2 * KG)))
                    sp.dma_start(CT[:, :, h - 1].rearrange("p b c k -> p b (c k)"),
                                 conv_d[h - 1].rearrange("b c r k n y -> (c r k) b (n y)")).then_inc(S["conv_in"], 16)
            sp.wait_ge(*nth("c_ready", 1))
            with sp.Fori(0, NU // 2) as t:
                for e in range(2):
                    sp.wait_ge(*nth("q_mm", t * 2 + e - 1))
                    sp.wait_ge(*nth("gram_used", t * 2 + e - 1))
                    sp.dma_start(crs[:, e, :, 0:W], xh_d[ds(t * 2 + e, 1)].rearrange("u p a w -> (u p) a w")
                                 ).then_inc(S[f"crs_in{e}"], 16)
                    sp.dma_start(gram_in[:, e], gram_d[ds(t * 2 + e, 1)].rearrange("u p a -> (u p) a")
                                 ).then_inc(S[f"gram_in{e}"], 16)
            sp.wait_ge(*nth("cov_ready", 1))
            sp.dma_start(cov_d.rearrange("p a b -> p (a b)"), cov[:, :]).then_inc(S["cov_stored"], 16)
            sp.wait_ge(*nth("cov_stored", 16))
            for half in range(2):
                for s in range(2):
                    for q in range(4):
                        g = 8 * half + 4 * s + q
                        row = BL * q + M * s
                        sp.dma_start(aug[g:g + 1, :, 0:M],
                                     cov_d[row:row + M, half, M * s:M * s + M].unsqueeze(0)
                                     ).then_inc(S["aug_in"], 16)
            sp.wait_ge(*nth("inv_ready", 1))
            sp.dma_start(inv_d, inv[:, :, :]).then_inc(S["inv_stored"], 16)
            sp.wait_ge(*nth("inv_stored", 16))
            sp.wait_ge(*nth("whit_zero", 1))
            for half in range(2):
                for s in range(2):
                    for q in range(4):
                        g = 8 * half + 4 * s + q
                        row = BL * q + M * s
                        sp.dma_start(whit[row:row + M, half, row:row + M], inv_d[g]).then_inc(S["whit_in"], 16)
            sp.wait_ge(*nth("ms_ready", 1))
            def load(t, j):
                sp.dma_start(x_re[:, 2 * j:2 * j + 2], x_v[:, ds(t * 8 + 2 * j, 2)]).then_inc(S[f"x_re_in{j}"], 16)

            def store(t, j):
                sp.wait_ge(*nth("o_ready", t * 8 + 2 * j + 2))
                sp.dma_start(out_v[:, ds(t * 8 + 2 * j, 2)],
                             o_sb[:, j].rearrange("p (c r) w -> p c r w", c=2)).then_inc(S[f"out_stored{j}"], 16)

            for j in range(4):
                load(0, j)
            with sp.Fori(1, NP // 4) as t:
                for j in range(4):
                    sp.wait_ge(*nth(f"x_re_used{j}", t))
                    load(t, j)
                    store(t - 1, j)
            for j in range(4):
                store(NP // 4 - 1, j)
            for j in range(4):
                sp.wait_ge(*nth(f"out_stored{j}", 16 * (NP // 4)))

        @block.tensor
        def _(pe):
            head_start(pe, "tensor")
            mm = nc.tensor.matmul
            pe.wait_ge(*nth("tab_in", 16))
            one = dict(start=True, stop=True)

            def products(u, q):
                if q % 2 == 0:
                    pe.wait_ge(*nth(f"x_in{q // 2}", u * 16 + 16))
                    pe.wait_ge(*nth("gram_copied", u * 4 + q // 2 - 1))
                for half in range(2):
                    for c in range(2):
                        for t in range(2):
                            blk = x_in[:, 2 * q + c, t, P * half:P * half + P]
                            at = W * (q % 2) + P * half
                            ins = mm(bank[q // 2 % 2][:, at:at + P], blk, blk, start=c == 0 and t == 0 and half == 0,
                                     stop=c == 1 and t == 1, skip_group_check=True)
                if q % 2 == 1:
                    ins.then_inc(S["gram_mm"], 1)
                pe.wait_ge(*nth("xh_copied", u * PAIRS + q - 1))
                for t in range(2):
                    for c in range(2):
                        ins = mm(bank[2 + q % 2][KH * c:KH * c + KH, 0:W], hc[:, t], x_in[:, 2 * q + c, t],
                                 start=t == 0, stop=t == 1)
                ins.then_inc(S["xh_mm"], 1)

            def transposes(u, q):
                pe.wait_ge(*nth("xt_copied", u * PAIRS + q - 1))
                pe.wait_ge(*nth("xh_copied", u * PAIRS + q + 1))
                for half in range(2):
                    ins = mm(bank[4 + q % 2][:, P * half:P * half + P], xh[:, q, P * half:P * half + P], T("eye"),
                             start=half == 0, stop=True, is_transpose=True, skip_group_check=True)
                ins.then_inc(S["xt_mm"], 1)

            def spectrum(u, q):
                pe.wait_ge(*nth("xt_copied", u * PAIRS + q + 1))
                if q == 0:
                    pe.wait_ge(*nth("d_copied", u))
                for half in range(2):
                    ins = mm(bank[6][:, KW * q:KW * q + KW], xht[:, q % 2, half], ew[:, half],
                             start=half == 0, stop=half == 1, skip_group_check=True)
                if q == PAIRS - 1:
                    ins.then_inc(S["d_mm"], 1)
                if q % 2 == 0:
                    ins.then_inc(S[f"x_used{q // 2}"], 1)

            def turned(u):
                pe.wait_ge(*nth("d_copied", u + 1))
                pe.wait_ge(*nth("rot_read", u))
                mm(bank[7][:, 0:PAIRS * KY].rearrange("p (n y) -> p n y", y=KY), T("rot"),
                   D[:, ds(u * PAIRS, PAIRS), KY:KW], **one).then_inc(S["rot_mm"], 1)

            def unit(u, first=False):
                for q in range(PAIRS):
                    products(u, q)
                    if q >= 1:
                        transposes(u, q - 1)
                    elif not first:
                        transposes(u - 1, PAIRS - 1)
                    if q >= 2:
                        spectrum(u, q - 2)
                    elif not first:
                        spectrum(u - 1, PAIRS - 2 + q)
                    if q == 4 and not first:
                        turned(u - 1)

            unit(0, first=True)
            with pe.Fori(1, NU) as u:
                unit(u)
            transposes(NU - 1, PAIRS - 1)
            spectrum(NU - 1, PAIRS - 2)
            spectrum(NU - 1, PAIRS - 1)
            turned(NU - 1)
            pe.wait_ge(*nth("spectra_ready", 1))
            mm(bank[0][:, 0:NP], T("mean"), D[:, :, 0], **one).then_inc(S["stat_mm"], 1)
            mm(bank[1][:, 0:NP], T("ones"), ssq_part[:, :], **one).then_inc(S["stat_mm"], 1)
            for h in range(HEADS):
                pe.wait_ge(*nth("signed", h + 1))
                for a in range(KA):
                    for part, (y0, y1) in enumerate(((0, 9), (9, KY))):
                        n = h * 2 * KA + 2 * a + part
                        if n >= 2:
                            pe.wait_ge(*nth("mode_act", n - 1))
                            pe.wait_ge(*nth("mode_dve", n - 1))
                        for y in range(y0, y1):
                            for g in range(KG):
                                r = slice(32 * g, 32 * g + 32)
                                ins = mm(bank[2 * g + part][32 * g:32 * g + B, 32 * (y - y0):32 * (y - y0) + 32],
                                         modes_in[r, h % 2, :, KY * a + y],
                                         weights[r, h % 2, :, :, KY * a + y].rearrange("p r o -> p (r o)"), **one)
                        ins.then_inc(S["mode_mm"], 1)
            pe.wait_ge(*nth("conv_in", 16 * HEADS))
            with pe.Fori(0, NP // 32) as t:
                for e in range(2):
                    pe.wait_ge(*nth("rot2_act", t * 2))
                    mm(bank[2 + e][:, 0:16 * KY], T("rot"),
                       CTf[:, ds(t * 32 + 16 * e, 16)].rearrange("p n y -> p (n y)"), **one).then_inc(S["rot2_mm"], 1)
            pe.wait_ge(*nth("c_ready", 1))
            mm(bank[0][:, 0:NP], T("mean"), C[:, :, 0], **one).then_inc(S["m1_mm"], 1)
            pe.wait_ge(*nth("var_ready", 1))
            mm(bank[1][:, 0:NP], T("ones"), tmp[:, :], **one).then_inc(S["var_mm"], 1)
            with pe.Fori(0, NU // 2) as t:
                for e in range(2):
                    pe.wait_ge(*nth(f"crs_in{e}", t * 16 + 16))
                    pe.wait_ge(*nth("cr_ready", t * 2 + e + 1))
                    pe.wait_ge(*nth("q_read", t * 2 + e - 1))
                    for q in range(PAIRS):
                        c = q % 2
                        ins = mm(bank[2 + e][KH * c:KH * c + KH, 0:W + KW], cr[:, e, q], crs[:, e, q],
                                 start=q < 2, stop=q >= PAIRS - 2)
                    ins.then_inc(S["q_mm"], 1)
            pe.wait_ge(*nth("qacc_ready", 1))
            nc.tensor.transpose(bank[0][0:KW, 0:P], qacc[:, W:W + KW], T("eye")).then_inc(S["qt_mm"], 1)
            pe.wait_ge(*nth("qt_ready", 1))
            mm(bank[1][0:KW + 1, 0:W], T("fold"), qacc[:, 0:W], start=True, stop=False)
            mm(bank[1][0:KW + 1, 0:W], qt[:, :], T("e0", KW), start=False, stop=True).then_inc(S["r_mm"], 1)
            pe.wait_ge(*nth("r_ready", 1))
            for half in range(2):
                for j in range(4):
                    w0 = P * half + BL * j
                    dst = bank[2][BL * j:BL * j + BL, BL * half:BL * half + BL]
                    e1 = T("e1", KW + 1)[:, w0:w0 + BL]
                    mm(dst, R[:, w0:w0 + BL], e1, start=half == 0, stop=False, skip_group_check=True)
                    mm(dst, e1, R[:, w0:w0 + BL], start=False, stop=False, skip_group_check=True)
                    ins = mm(dst, sneg[0:1, w0:w0 + BL], R[0:1, w0:w0 + BL], start=False, stop=True,
                             skip_group_check=True)
            ins.then_inc(S["cov_mm"], 1)
            for half in range(2):
                ins = mm(bank[3][:, P * half:P * half + P], R[0:1, P * half:P * half + P], T("ones", 1), start=half == 0,
                         stop=True, skip_group_check=True)
            ins.then_inc(S["ms_mm"], 1)
            pe.wait_ge(*nth("ms_ready", 1))
            pe.wait_ge(*nth("whit_in", 16 * 16))
            for half in range(2):
                ins = mm(bank[4][:, P * half:P * half + P], msum[:, half], whit[:, half], start=half == 0, stop=True,
                         skip_group_check=True)
            ins.then_inc(S["mw_mm"], 1)
            pe.wait_ge(*nth("mw_ready", 1))
            def expand(t, q):
                pe.wait_ge(*nth("cs_ready", t * 4 + q + 1))
                pe.wait_ge(*nth("v_copied", t * 4 + q - 1))
                mm(bank[q % 2][0:KW, :], cs[:, q], T("hb"), **one).then_inc(S["v_mm"], 1)

            def turn(t, q):
                pe.wait_ge(*nth(f"x_re_in{q}", t * 16 + 16))
                for half in range(2):
                    pe.wait_ge(*nth("xt2_copied", t * 8 + 2 * q + half - 1))
                    for c in range(2):
                        for r in range(2):
                            mm(bank[2 + half][:, H * c + P * r:H * c + P * r + P],
                               x_re[:, 2 * q + c, r, P * half:P * half + P], T("eye"), start=c == 0 and r == 0,
                               stop=False, is_transpose=True, skip_group_check=True)
                    pe.wait_ge(*nth("v_copied", t * 4 + q + 1))
                    mm(bank[2 + half][:, :], T("e0", KW)[:, P * half:P * half + P], v_sb[0:KW, q % 2],
                       start=False, stop=True, skip_group_check=True).then_inc(S["xt2_mm"], 1)

            def whitened(t, q):
                e = q % 2
                pe.wait_ge(*nth("w_ready", t * 4 + q + 1))
                pe.wait_ge(*nth("xt2_copied", t * 8 + 2 * q + 2))
                for c in range(2):
                    pe.wait_ge(*nth("o_ready", t * 8 + 2 * q + c - 3))
                    for r in range(2):
                        for half in range(2):
                            ins = mm(bank[4 + 2 * e + c][:, W * r + P * half:W * r + P * half + P],
                                     xt_sb[:, e, half, H * c + P * r:H * c + P * r + P], wp[:, e, half],
                                     start=r == 0 and half == 0, stop=True, skip_group_check=True)
                            if c == 0 and r == 0 and half == 0:
                                ins.then_inc(S[f"x_re_used{q}"], 1)
                    ins.then_inc(S["o_mm"], 1)

            def four(t, first=False, last=False):
                for q in range(4):
                    turn(t, q)
                    if q < 3:
                        expand(t, q + 1)
                    elif not last:
                        expand(t + 1, 0)
                    if q >= 1:
                        whitened(t, q - 1)
                    elif not first:
                        whitened(t - 1, 3)

            expand(0, 0)
            four(0, first=True)
            with pe.Fori(1, NP // 4 - 1) as t:
                four(t)
            four(NP // 4 - 1, last=True)
            whitened(NP // 4 - 1, 3)

        def root(act, n, a):
            act.wait_ge(*nth("root_wanted", n))
            nc.scalar.activation(root_out[0:a.shape[0], 0:a.shape[1]], a, ACT.Sqrt).then_inc(S["root_done"], 1)

        @block.scalar
        def _(act):
            head_start(act, "scalar")
            copy = lambda o, i, **k: nc.scalar.activation(o, i, ACT.Copy, **k)
            with act.Fori(0, NU) as u:
                for q in range(PAIRS):
                    if q % 4 == 0:
                        act.wait_ge(*nth(f"xh_out{q // 4}", u * 16))
                    act.wait_ge(*nth("xh_mm", u * PAIRS + q + 1))
                    copy(xh[:, q], bank[2 + q % 2][:, 0:W]).then_inc(S["xh_copied"], 1)
                    if q % 2 == 1:
                        j = q // 2
                        if j == 0:
                            act.wait_ge(*nth("gram_out", u * 16))
                            act.wait_ge(*nth("diag_done", u))
                        act.wait_ge(*nth("gram_mm", u * 4 + j + 1))
                        for i in range(4):
                            r = slice(BL * i, BL * i + BL)
                            ins = copy(gram[r, 2 * j:2 * j + 2].rearrange("p n (f b) -> p (n f) b", f=2),
                                       bank[j % 2][r, :].rearrange("p (n b) -> p n b", b=P)[:, :, BL * i:BL * i + BL])
                        ins.then_inc(S["gram_copied"], 1)
                    if q % 4 == 3:
                        j = q // 4
                        act.wait_ge(*nth("xh_copied", u * PAIRS + q + 1))
                        act.dma_start(xh_d[ds(u, 1), :, 4 * j:4 * j + 4].rearrange("u p a w -> (u p) a w"),
                                      xh[:, 4 * j:4 * j + 4]).then_inc(S[f"xh_out{j}"], 16)
                act.wait_ge(*nth("gram_copied", u * 4 + 4))
                act.dma_start(gram_d[ds(u, 1)].rearrange("u p a -> (u p) a"),
                              flat(gram[:, :, :])).then_inc(S["gram_out"], 16)
            root(act, 1, root_in[:, :])
            for h in range(HEADS):
                if h >= 1:
                    act.wait_ge(*nth("conv_stored", h * (16 * 2 * KG)))
                for a in range(KA):
                    for part, (y0, y1) in enumerate(((0, 9), (9, KY))):
                        act.wait_ge(*nth("mode_mm", h * 2 * KA + 2 * a + part + 1))
                        for g in range(2):
                            ins = copy(modes_out[32 * g:32 * g + B, :, a, :, y0:y1],
                                       bank[2 * g + part][32 * g:32 * g + B, 0:32 * (y1 - y0)].rearrange(
                                           "p (y r n) -> p r n y", r=4, n=PAIRS))
                        ins.then_inc(S["mode_act"], 1)
            with act.Fori(0, NP // 32) as t:
                for e in range(2):
                    act.wait_ge(*nth("rot2_mm", t * 2 + e + 1))
                    copy(C[:, ds(t * 32 + 16 * e, 16), KY:KW],
                         bank[2 + e][:, 0:16 * KY].rearrange("p (n y) -> p n y", y=KY),
                         scale=-1.0).then_inc(S["rot2_act"], 1)
            root(act, 2, root_in[:, :])
            act.wait_ge(*nth("qt_mm", 1))
            copy(qtp[:, :], bank[0][0:KW, 0:P]).then_inc(S["act_chain"], 1)
            act.wait_ge(*nth("ms_mm", 1))
            copy(msum[:, :, :].rearrange("p a b -> p (a b)"), bank[3][:, 0:W]).then_inc(S["ms_ready"], 1)
            root(act, 3, root_in[0:M, 0:M])
            act.wait_ge(*nth("mw_mm", 1))
            copy(mwhit[:, :], bank[4][:, 0:W], scale=1.0 / ROWS).then_inc(S["mw_ready"], 1)
            def scaled(t, q):
                act.wait_ge(*nth("w_ready", t * 4 + q - 1))
                copy(wr[:, q % 2].rearrange("p a b -> p (a b)"), flat(whit[:, :, :]),
                     scale=r1[:, ds(t * 4 + q, 1)]).then_inc(S["w_scaled"], 1)

            def expanded(t, q):
                act.wait_ge(*nth("v_mm", t * 4 + q + 1))
                act.wait_ge(*nth("xt2_mm", t * 8 + 2 * q - 2))
                copy(v_sb[0:KW, q % 2], bank[q % 2][0:KW, :]).then_inc(S["v_copied"], 1)

            def four(t, last=False):
                for q in range(4):
                    act.wait_ge(*nth("o_mm", t * 8 + 2 * q - 2))
                    for half in range(2):
                        act.wait_ge(*nth("xt2_mm", t * 8 + 2 * q + half + 1))
                        copy(xt_sb[:, q % 2, half], bank[2 + half][:, :]).then_inc(S["xt2_copied"], 1)
                    if not (last and q == 3):
                        n, m = (t, q + 1) if q < 3 else (t + 1, 0)
                        expanded(n, m)
                        scaled(n, m)

            scaled(0, 0)
            expanded(0, 0)
            with act.Fori(0, NP // 4 - 1) as t:
                four(t)
            four(NP // 4 - 1, last=True)

        @block.gpsimd
        def _(pool):
            head_start(pool, "gpsimd")
            pch = Chain(pool, S["pool_chain"])
            pch(nc.gpsimd.memset(beta[:, :], 0.0))
            pool.sem_inc(S["beta_zero"], 1)
            pch(nc.gpsimd.memset(whit[:, :, :], 0.0))
            pool.sem_inc(S["whit_zero"], 1)
            pool.wait_ge(*nth("r1_ready", 1))
            pch(nc.gpsimd.memset(gacc, 0.0))
            pch.enter(None, 0)
            with pool.Fori(0, NU // 2) as t:
                pch.enter(t, 4)
                for e in range(2):
                    pool.wait_ge(*nth(f"gram_in{e}", t * 16 + 16))
                    g3 = lambda a: a.rearrange("p (n b) -> p n b", b=2 * BL)
                    pch(nc.gpsimd.tensor_tensor(
                        out=g3(gram_w), in0=g3(gram_in[:, e]),
                        in1=r1sq[:, ds((t * 2 + e) * PAIRS, PAIRS)].unsqueeze(2).to_broadcast([P, PAIRS, 2 * BL]),
                        op=ALU.mult))
                    pch(nc.gpsimd.tensor_tensor(out=gacc, in0=gacc, in1=gram_w, op=ALU.add))
                    pool.sem_inc(S["gram_used"], 1)
            pch.leave(NU // 2)
            pool.wait_ge(*nth("mw_ready", 1))
            with pool.Fori(0, NP // 4) as t:
                for q in range(4):
                    e = q % 2
                    pool.wait_ge(*nth("v_mm", t * 4 + q - 3))
                    nc.gpsimd.tensor_copy(cs[:, q], C[:, ds(t * 4 + q, 1)].rearrange("p a b -> p (a b)")
                                          ).then_inc(S["cs_ready"], 1)
                    pool.wait_ge(*nth("w_scaled", t * 4 + q + 1))
                    pool.wait_ge(*nth("o_mm", t * 8 + 2 * q - 2))
                    nc.gpsimd.tensor_tensor(out=wp[:, e], in0=wr[:, e],
                                            in1=T("eye").unsqueeze(1).to_broadcast([P, 2, P]),
                                            op=ALU.add).then_inc(S["w_ready"], 1)

        @block.vector
        def _(dve):
            head_start(dve, "vector")
            v = nc.vector
            ch = Chain(dve, S["dve_chain"])

            def inverse_root(n, r, a):
                dve.sem_inc(S["root_wanted"], 1)
                dve.wait_ge(*nth("root_done", n))
                t = root_out[0:a.shape[0], 0:a.shape[1]]
                ch(v.reciprocal(r, t))
                ch(v.tensor_tensor(out=t, in0=r, in1=r, op=ALU.mult))
                ch(v.tensor_tensor(out=t, in0=t, in1=a, op=ALU.mult))
                ch(v.tensor_scalar(t, t, -0.5, 1.5, ALU.mult, ALU.add))
                ch(v.tensor_tensor(out=r, in0=r, in1=t, op=ALU.mult))

            dve.wait_ge(*nth("tab_in", 16))

            def unit(u, first=False):
                for q in range(PAIRS):
                    dve.wait_ge(*nth("xt_mm", u * PAIRS + q + 1))
                    v.tensor_copy(xht[:, q % 2].rearrange("p a b -> p (a b)"),
                                  bank[4 + q % 2][:, 0:W]).then_inc(S["xt_copied"], 1)
                    if q == 5 and not first:
                        turned(u - 1)
                dve.wait_ge(*nth("d_mm", u + 1))
                v.tensor_copy(D[:, ds(u * PAIRS, PAIRS)].rearrange("p a b -> p (a b)"),
                              bank[6][:, 0:PAIRS * KW]).then_inc(S["d_copied"], 1)
                dve.wait_ge(*nth("gram_copied", u * 4 + 4))
                ch(v.tensor_tensor(out=gmask[:, :, :], in0=gram[:, :, :],
                                   in1=T("eye32").unsqueeze(1).to_broadcast([P, PAIRS, 2 * BL]), op=ALU.mult))
                ch(v.tensor_reduce(out=ssq_part[:, ds(u * PAIRS, PAIRS)], in_=gmask[:, :, :], axis=AX.X, op=ALU.add))
                dve.sem_inc(S["diag_done"], 1)

            def turned(u):
                dve.wait_ge(*nth("rot_mm", u + 1))
                dve.wait_ge(*nth("ps_stored", 64 * u))
                v.tensor_tensor(out=psu[:, :, :], in0=bank[7][:, 0:PAIRS * KY].rearrange("p (n y) -> p n y", y=KY),
                                in1=D[:, ds(u * PAIRS, PAIRS), 0:KY], op=ALU.add).then_inc(S["rot_read"], 1)

            unit(0, first=True)
            with dve.Fori(1, NU) as u:
                ch.enter(u - 1, 2)
                unit(u)
            ch.leave(NU - 1)
            turned(NU - 1)
            dve.wait_ge(*nth("d_copied", NU))
            dve.sem_inc(S["spectra_ready"], 1)
            for n in ("xh_out0", "xh_out1", "gram_out"):
                dve.wait_ge(*nth(n, 16 * NU))
            dve.wait_ge(*nth("stat_mm", 2))
            ch(v.tensor_copy(m0[:, :], bank[0][:, 0:NP]))
            ch(v.tensor_copy(ssq[:, :], bank[1][:, 0:NP]))
            ch(v.tensor_tensor(out=tmp[:, :], in0=m0[:, :], in1=m0[:, :], op=ALU.mult))
            ch(v.scalar_tensor_tensor(out=r0[:, :], in0=ssq[:, :], scalar=1.0 / GROUP, in1=tmp[:, :],
                                      op0=ALU.mult, op1=ALU.subtract))
            ch(v.tensor_scalar(root_in[:, :], r0[:, :], EPS_GN, None, ALU.add))
            inverse_root(1, r0[:, :], root_in[:, :])
            for src, dst in ((m0[:, :], m0_row), (r0, r0_row)):
                ch(v.tensor_tensor(out=pick, in0=src.rearrange("p (u n) -> p u n", n=PAIRS),
                                   in1=T("pick").unsqueeze(1).to_broadcast([P, NU, PAIRS]), op=ALU.mult))
                ch(v.tensor_reduce(out=dst, in_=pick, axis=AX.X, op=ALU.add))
            ch(v.tensor_scalar(m0_row, m0_row, T("dcrow"), None, ALU.mult))

            def sign(h):
                dve.wait_ge(*nth(f"weights_in{h % 2}", (h // 2 + 1) * (16 * 32)))
                ch(v.tensor_scalar(weights[:, h % 2, 1], weights[:, h % 2, 1], T("sgn"), None, ALU.mult))
                dve.wait_ge(*nth(f"modes_in_in{h % 2}", (h // 2 + 1) * 16 * KG))
                mi = modes_in[:, h % 2]
                ch(v.tensor_tensor(out=mi[:, :, 0], in0=mi[:, :, 0], in1=m0_row[:, h:NU:HEADS], op=ALU.add))
                ch(v.tensor_tensor(out=mi, in0=mi, in1=r0_row[:, h:NU:HEADS].unsqueeze(2).to_broadcast(
                    [P, B, KA * KY]), op=ALU.mult))
                dve.sem_inc(S["signed"], 1)

            sign(0)
            for h in range(HEADS):
                if h >= 1:
                    dve.wait_ge(*nth("conv_stored", h * (16 * 2 * KG)))
                for a in range(KA):
                    if a == 4 and h + 1 < HEADS:
                        sign(h + 1)
                    for part, (y0, y1) in enumerate(((0, 9), (9, KY))):
                        dve.wait_ge(*nth("mode_mm", h * 2 * KA + 2 * a + part + 1))
                        for g in range(2, 4):
                            ins = v.tensor_copy(modes_out[32 * g:32 * g + B, :, a, :, y0:y1],
                                                bank[2 * g + part][32 * g:32 * g + B, 0:32 * (y1 - y0)].rearrange(
                                                    "p (y r n) -> p r n y", r=4, n=PAIRS))
                        ins.then_inc(S["mode_dve"], 1)
            dve.wait_ge(*nth("conv_in", 16 * HEADS))
            dve.wait_ge(*nth("conv_stored", HEADS * 16 * 2 * KG))
            ch(v.tensor_copy(C[:, :, 0:KY], CTf))
            dve.wait_ge(*nth("beta_in", 32))
            b0 = C[:, :, 0].rearrange("p (b n) -> p b n", n=HEADS * PAIRS)
            ch(v.scalar_tensor_tensor(out=b0, in0=beta[:, :].unsqueeze(1).to_broadcast([P, B, HEADS * PAIRS]),
                                      scalar=float(AREA), in1=b0, op0=ALU.mult, op1=ALU.add))
            dve.wait_ge(*nth("rot2_act", NP // 16))
            dve.sem_inc(S["c_ready"], 1)
            dve.wait_ge(*nth("m1_mm", 1))
            ch(v.tensor_tensor(out=m1[:, :], in0=bank[0][:, 0:NP], in1=m0[:, :], op=ALU.add))
            ch(v.tensor_scalar(tmp[:, :], m1[:, :], T("dc"), -float(AREA), ALU.mult, ALU.mult))
            ch(v.tensor_tensor(out=C[:, :, 0], in0=C[:, :, 0], in1=tmp[:, :], op=ALU.add))
            for n in range(0, NP, 15):
                s = slice(n, min(n + 15, NP))
                k = s.stop - s.start
                wk = work[:, 0:k]
                ch(v.scalar_tensor_tensor(out=wk, in0=C[:, s], scalar=T("hk"), in1=D[:, s], op0=ALU.mult, op1=ALU.add))
                ch(v.tensor_tensor(out=wk, in0=wk, in1=C[:, s], op=ALU.mult))
                ch(v.tensor_tensor(out=wk, in0=wk, in1=T("weigh").unsqueeze(1).to_broadcast([P, k, KW]), op=ALU.mult))
                ch(v.tensor_reduce(out=tmp[:, s], in_=wk, axis=AX.X, op=ALU.add))
            dve.sem_inc(S["var_ready"], 1)
            dve.wait_ge(*nth("var_mm", 1))
            ch(v.tensor_tensor(out=r1[:, :], in0=bank[1][:, 0:NP], in1=ssq[:, :], op=ALU.add))
            ch(v.tensor_scalar(root_in[:, :], r1[:, :], 1.0 / GROUP, EPS_GN, ALU.mult, ALU.add))
            inverse_root(2, r1[:, :], root_in[:, :])
            ch(v.tensor_tensor(out=r1sq[:, :], in0=r1[:, :], in1=r1[:, :], op=ALU.mult))
            ch(v.memset(qacc, 0.0))
            ch(v.memset(cr.rearrange("p a b c -> p (a b c)"), 0.0))
            dve.sem_inc(S["r1_ready"], 1)
            with dve.Fori(0, NU // 2) as t:
                ch.enter(t, 8)
                for e in range(2):
                    n = ds((t * 2 + e) * PAIRS, PAIRS)
                    dve.wait_ge(*nth("q_mm", t * 2 + e - 1))
                    ch(v.tensor_scalar(crs[:, e, :, W:W + KW], C[:, n], T("hh"), None, ALU.mult))
                    ch(v.tensor_tensor(out=cr[:, e, :, 1:KW + 1], in0=C[:, n],
                                       in1=r1sq[:, n].unsqueeze(2).to_broadcast([P, PAIRS, KW]), op=ALU.mult))
                    ch(v.tensor_scalar(cr[:, e, :, 0], r1[:, n], T("dc"), None, ALU.mult))
                    dve.sem_inc(S["cr_ready"], 1)
                for e in range(2):
                    dve.wait_ge(*nth("q_mm", t * 2 + e + 1))
                    ch(v.tensor_tensor(out=qacc, in0=bank[2 + e][:, 0:W + KW], in1=qacc, op=ALU.add))
                    dve.sem_inc(S["q_read"], 1)
            ch.leave(NU // 2)
            dve.sem_inc(S["qacc_ready"], 1)
            dve.wait_ge(*nth("act_chain", 1))
            ch(v.tensor_tensor(out=qt[:, :], in0=qtp[:, 0:KW + 1], in1=qtp[:, KH:KH + KW + 1], op=ALU.add))
            ch(v.tensor_scalar(qt[:, 0:1], qt[:, 0:1], 2.0, None, ALU.mult))
            dve.sem_inc(S["qt_ready"], 1)
            dve.wait_ge(*nth("r_mm", 1))
            ch(v.tensor_copy(R[:, :], bank[1][0:KW + 1, 0:W]))
            ch(v.tensor_scalar(sneg[:, :], R[0:1, :], -1.0 / ROWS, None, ALU.mult))
            dve.sem_inc(S["r_ready"], 1)
            dve.wait_ge(*nth("gram_used", NU))
            ch(v.tensor_reduce(out=covg[:, :], in_=gacc.rearrange("p (n b) -> p b n", b=2 * BL), axis=AX.X,
                               op=ALU.add))
            dve.wait_ge(*nth("cov_mm", 1))
            ch(v.tensor_tensor(out=cov[:, :], in0=bank[2][:, 0:2 * BL], in1=covg[:, :], op=ALU.add))
            ch(v.tensor_scalar(cov[:, :], cov[:, :], (1.0 - EPS_W) / DENOM / DENOM, None, ALU.mult))
            ch(v.scalar_tensor_tensor(out=cov[:, :], in0=T("eye32"), scalar=EPS_W / DENOM, in1=cov[:, :],
                                      op0=ALU.mult, op1=ALU.add))
            dve.sem_inc(S["cov_ready"], 1)
            ch(v.memset(aug[:, :, M:2 * M], 0.0))
            diag = aug[:, :, :].rearrange("p a b -> p (a b)")
            ch(v.memset(diag[:, M:M + (2 * M + 1) * (M - 1) + 1:2 * M + 1], 1.0))
            dve.wait_ge(*nth("aug_in", 16 * 16))
            for j in range(M - 1):
                n = M - 1 - j
                ch(v.reciprocal(fac[:, 0:1], aug[:, j, j:j + 1]))
                ch(v.tensor_scalar(fac[:, 1:1 + n], aug[:, j + 1:M, j], fac[:, 0:1], None, ALU.mult))
                ch(v.tensor_tensor(out=step_[:, 0:n], in0=aug[:, j, :].unsqueeze(1).to_broadcast([M, n, 2 * M]),
                                   in1=fac[:, 1:1 + n].unsqueeze(2).to_broadcast([M, n, 2 * M]), op=ALU.mult))
                ch(v.tensor_tensor(out=aug[:, j + 1:M], in0=aug[:, j + 1:M], in1=step_[:, 0:n], op=ALU.subtract))
            ch(v.tensor_copy(root_in[0:M, 0:M], diag[:, 0:(2 * M + 1) * (M - 1) + 1:2 * M + 1]))
            inverse_root(3, fac[:, :], root_in[0:M, 0:M])
            ch(v.tensor_tensor(out=inv[:, :, :], in0=aug[:, :, M:2 * M].rearrange("p m k -> p k m"),
                               in1=fac[:, :].unsqueeze(1).to_broadcast([M, M, M]), op=ALU.mult))
            dve.sem_inc(S["inv_ready"], 1)
            dve.wait_ge(*nth("mw_ready", 1))
            with dve.Fori(0, NP // 4) as t:
                for q in range(4):
                    e = q % 2
                    dve.wait_ge(*nth(f"out_stored{q}", t * 16))
                    for c in range(2):
                        dve.wait_ge(*nth("o_mm", t * 8 + 2 * q + c + 1))
                        v.scalar_tensor_tensor(
                            out=o_sb[:, q, 2 * c:2 * c + 2],
                            in0=bank[4 + 2 * e + c][:, :].rearrange("p (r w) -> p r w", r=2),
                            scalar=m1[:, ds(t * 4 + q, 1)],
                            in1=mwhit[:, :].unsqueeze(1).to_broadcast([P, 2, W]),
                            op0=ALU.add, op1=ALU.subtract).then_inc(S["o_ready"], 1)


_INS = ["x", "L0_conv_weight_re", "L0_conv_weight_im", "L0_conv_bias"]


def kernel(**inputs):
    import concourse.bacc as _bacc
    from concourse.bass_utils import run_bass_kernel_spmd as _run

    nc = _bacc.Bacc("TRN2", target_bir_lowering=False, num_devices=1)
    arrays, args = {}, []
    for name in _INS:
        a = np.ascontiguousarray(inputs[name])
        arrays[f"in_{name}_dram"] = a
        args.append(nc.dram_tensor(f"in_{name}_dram", a.shape, mybir.dt.from_np(a.dtype), kind="ExternalInput").ap())
    table = tables()
    arrays["table_dram"] = table
    args.append(nc.dram_tensor("table_dram", table.shape, mybir.dt.float32, kind="ExternalInput").ap())
    shape = tuple(inputs["x"].shape)
    args.append(nc.dram_tensor("out_0_dram", shape, mybir.dt.float32, kind="ExternalOutput").ap())
    whiten_kernel(nc, *args)
    r = _run(nc, [arrays], core_ids=[0])
    return r.results[0]["out_0_dram"]
```

```python
import concourse.bass as bass
from concourse import mybir
from contextlib import ExitStack
import numpy as np

P = 128
HEADS, HC = 4, 16
PAIRS = HC // 2
H = W = 256
KX, KY = 32, 17
KH, KW = 2 * KX, 2 * KY
KG, KA = 4, 8
AREA = H * W
GROUP = 2 * AREA
M = 16
BL = 32
EPS_GN, EPS_W = 1e-5, 1e-3
NI = KX // 2

COLS = dict(cut1=1, cut2=1, hc=KH, ew=2 * BL, hb=2 * H, e0=W, e1=W, rot=P, fold=KW + 1, eye=P, eye32=2 * BL, dc=1, hk=1, hh=1,
            sgn=1, dcrow=1, pick=PAIRS, ones=P, mean=P)


def columns():
    at, out = 0, {}
    for name, n in COLS.items():
        out[name] = (at, at + n)
        at += n
    return out, at


def parts(a):
    out = []
    for _ in range(3):
        bits = a.astype(np.float32).view(np.uint32).astype(np.uint64)
        high = ((bits + 0x7FFF + ((bits >> 16) & 1)) & 0xFFFF0000).astype(np.uint32).view(np.float32)
        out.append(high)
        a = a.astype(np.float32) - high
    return out


def tables():
    where, n = columns()
    t = np.zeros((P, n), np.float64)

    def put(name, a, rows=slice(0, P)):
        t[rows, where[name][0]:where[name][1]] = a.reshape(a.shape[0], -1)

    th = 2 * np.pi / H
    hk = np.concatenate([np.cos(th * np.outer(np.arange(KX), np.arange(H))),
                         np.sin(th * np.outer(np.arange(KX), np.arange(H)))])
    wj = np.concatenate([np.cos(th * np.outer(np.arange(KY), np.arange(W))),
                         np.sin(th * np.outer(np.arange(KY), np.arange(W)))])
    cj = np.tile(np.where(np.arange(KY) == 0, 1.0, 2.0), 2) / AREA
    cj[KY] = 0.0
    par, chan, trig, i = np.unravel_index(np.arange(P), (2, 2, 2, NI))
    kx = 2 * i + par
    hk_row = hk[trig * KX + kx]
    put("hc", hk_row.reshape(2, 2, 2 * NI, H)[:, 0, :, 0:P].transpose(2, 0, 1))
    ew = np.zeros((P, 2, 2, BL // 2))
    for par in range(2):
        ew[:, par, :, 0:(KY + 1 - par) // 2] = wj.reshape(2, KY, W)[:, par::2, 0:P].transpose(2, 0, 1)
    put("ew", ew)
    hb = hk_row[:, None, :] * (chan[:, None] == np.arange(2))[:, :, None]
    put("hb", hb.reshape(P, 2 * H))
    put("e0", cj[:, None] * wj, slice(0, KW))
    put("e1", cj[:, None] * wj, slice(1, KW + 1))
    rot = np.zeros((P, P))
    for r in range(P):
        rot[r, r + NI if trig[r] == 0 else r - NI] = 1.0 if trig[r] == 0 else -1.0
    put("rot", rot)
    fold = np.zeros((P, KW + 1))
    fold[np.arange(KW + 1), np.arange(KW + 1)] = 1.0
    fold[KH + np.arange(KW + 1), np.arange(KW + 1)] = 1.0
    put("fold", fold)
    put("eye", np.eye(P))
    put("eye32", np.tile(np.eye(BL), (P // BL, 2)))
    dc = np.zeros((P, 1))
    dc[(kx == 0) & (trig == 0)] = 1.0
    put("dc", dc)
    norm = np.where(kx > 0, H / 2, np.where(trig == 0, H, 0))[:, None]
    put("hk", norm / (2 * H))
    put("hh", norm / 2)
    put("sgn", np.tile(np.repeat([-1.0, 1.0], HC), KG)[:, None])
    rows = np.arange(P)
    put("dcrow", np.where(rows < HC, -float(AREA), 0.0)[:, None])
    put("pick", (rows[:, None] // 2 % PAIRS == np.arange(PAIRS)).astype(float))
    put("ones", np.ones((P, P)))
    put("cut1", np.repeat([0.0, -1.0, -1.0], KW)[:, None], slice(0, 3 * KW))
    put("cut2", np.repeat([0.0, 0.0, -1.0], KW)[:, None], slice(0, 3 * KW))
    put("mean", np.repeat(dc, P, 1) / GROUP)
    e = parts(cj[:, None] * wj)
    y = np.zeros((P, 2, W), np.float32)
    y[0:3 * KW, 0] = np.concatenate([e[0], e[0], e[0]])
    y[0:3 * KW, 1] = np.concatenate([e[1], e[2], e[1]])
    return np.concatenate([t.astype(np.float32), y.reshape(P, 2 * W)], 1)


class Chain:

    def __init__(self, eng, sem):
        self.eng, self.sem, self.n, self.i, self.k, self.n0 = eng, sem, 0, None, 0, 0

    def value(self):
        return self.n if self.i is None else self.i * self.k + self.n

    def __call__(self, ins):
        ins.then_inc(self.sem, 1)
        self.n += 1
        self.eng.wait_ge(self.sem, self.value())

    def enter(self, i, k):
        self.i, self.k, self.n0 = i, k, self.n

    def leave(self, trips):
        assert self.n - self.n0 == self.k, (self.n, self.n0, self.k)
        self.n, self.i = self.n0 + self.k * trips, None


def whiten_kernel(nc, x, w_re, w_im, bias, table, out):
    f32, bf16 = mybir.dt.float32, mybir.dt.bfloat16
    ALU, ACT, AX = mybir.AluOpType, mybir.ActivationFunctionType, mybir.AxisListType
    B = x.shape[0]
    NU, NP = B * HEADS, B * HEADS * PAIRS
    ROWS = B * HEADS * HC * H
    DENOM = ROWS - 1.0
    where, ncols = columns()
    ds = bass.ds

    x_v = x.rearrange("b c (t p) w -> p (b c) t w", p=P)
    out_v = out.rearrange("b c (t p) w -> p (b c) t w", p=P)

    xh_d = nc.dram_tensor("xh_d", (NU, P, PAIRS, W), f32, kind="Internal").ap()
    gram_d = nc.dram_tensor("gram_d", (NU, P, PAIRS * 2 * BL), f32, kind="Internal").ap()
    spec_d = nc.dram_tensor("spec_d", (2, PAIRS, 2, NU, KX, KY), f32, kind="Internal").ap()
    conv_d = nc.dram_tensor("conv_d", (HEADS, B, 2, 2, KX, PAIRS, KY), f32, kind="Internal").ap()
    cov_d = nc.dram_tensor("cov_d", (P, 2, BL), f32, kind="Internal").ap()
    inv_d = nc.dram_tensor("inv_d", (2 * W // BL, M, M), f32, kind="Internal").ap()

    ctx = ExitStack()
    with ctx:
        def sb(name, shape):
            return ctx.enter_context(nc.sbuf_tensor(name, shape, f32))

        def sem(name):
            return ctx.enter_context(nc.semaphore(name))

        bank = [ctx.enter_context(nc.psum_tensor(f"bank{i}", [P, 512], f32)) for i in range(8)]
        tab = sb("tab", [P, ncols])
        reg1 = sb("reg1", [P, NP * KW])
        reg2 = sb("reg2", [P, max(NP * KW, 3 * 4352 + 2 * B * 136)])
        reg3 = sb("reg3", [P, max(NP * KY, 8192 + 512)])

        def T(name, rows=P):
            a, b = where[name]
            return tab[0:rows, a:b]

        def cut(reg, at, *shape):
            n = int(np.prod(shape))
            v = reg[:, at:at + n]
            if len(shape) > 1:
                names = [f"d{i}" for i in range(len(shape))]
                v = v.rearrange(f"p ({' '.join(names)}) -> p {' '.join(names)}",
                                **{k: s for k, s in zip(names[1:], shape[1:])})
            return v, at + n

        hc = T("hc").rearrange("p (a k) -> p a k", a=2)
        ew = T("ew").rearrange("p (a j) -> p a j", a=2)

        D, _ = cut(reg1, 0, NP, KW)
        C, _ = cut(reg2, 0, NP, KW)
        weights, a = cut(reg2, 0, 2, 2, HC, KA * KY)
        modes_in, a = cut(reg2, a, 2, B, KA * KY)
        halves, b = cut(reg2, a, 2, 2, 2, W)
        xw, b = cut(reg2, b, 2, 2, P)
        dt, _ = cut(reg2, b, P)
        modes_out, a = cut(reg2, a, 4, KA, PAIRS, KY)
        x_in, _ = cut(reg3, 0, 16, 2, W)
        CTf, _ = cut(reg3, 0, NP, KY)
        CT = CTf.rearrange("p (b h c) k -> p b h c k", h=HEADS, c=PAIRS)
        VN = min(64, NP // 2)
        work, _ = cut(reg3, 0, 2, VN, KW)
        crs, a = cut(reg3, 0, 2, PAIRS, W + KW)
        gram_in, a = cut(reg3, a, 2, PAIRS * 2 * BL)
        gram_w, a = cut(reg3, a, PAIRS * 2 * BL)
        cr, a = cut(reg3, a, 2, PAIRS, KH)
        x_re, _ = cut(reg3, 0, 16, 2, W)

        xh = sb("xh", [P, PAIRS, W])
        psu = sb("psu", [P, PAIRS, KY])
        xht = sb("xht", [P, 4, 2, P])
        gram = sb("gram", [P, PAIRS, 2 * BL])
        gmask = sb("gmask", [P, PAIRS, 2 * BL])
        ssq_part = sb("ssq_part", [P, NP])
        flat = lambda t: t.rearrange("p a b -> p (a b)")
        xh_f, xht_f, gmask_f = flat(xh[:, :, :]), xht[:, 0:2].rearrange("p a b c -> p (a b c)"), flat(gmask[:, :, :])
        root_in, root_out = (xh_f[:, i * NP:i * NP + NP] for i in range(2))
        r0 = xh_f[:, 2 * 512:2 * 512 + NP]
        aug = xh_f[0:M, 3 * 512:4 * 512].rearrange("p (a b) -> p a b", a=M)
        step_ = xht_f[0:M, :].rearrange("p (a b) -> p a b", a=M)
        pick = gmask_f[:, 0:NP].rearrange("p (u n) -> p u n", n=PAIRS)
        m0_row, r0_row = xht_f[:, 0:NU], xht_f[:, NU:2 * NU]
        ey_f = xh_f[:, 2 * 512:3 * 512]
        sneg = xht_f[0:1, 0:W]
        inv = gmask_f[0:M, 0:M * M].rearrange("p (a b) -> p a b", a=M)
        m0, ssq, tmp = sb("m0", [P, NP]), sb("ssq", [P, NP]), sb("tmp", [P, NP])
        m1, r1, r1sq = m0, ssq, ssq_part
        beta = sb("beta", [P, HEADS * PAIRS])
        qacc, a = cut(reg3, a, W + KW)
        gacc, a = cut(reg3, a, PAIRS * 2 * BL)
        R, a = cut(reg3, a, W)
        R = R[0:KW + 1]
        qt, qtp = sb("qt", [KW, KW + 1]), sb("qtp", [KW, P])
        cov, covg = sb("cov", [P, 2 * BL]), sb("covg", [P, 2 * BL])
        fac = sb("fac", [M, M])
        whit, msum, mwhit = sb("whit", [P, 2, P]), sb("msum", [P, 2, P]), sb("mwhit", [P, W])

        def half_words(a, n):
            return a.bitcast(bf16).rearrange("p (n w) -> p n w", n=n)

        o_sb, a = cut(reg1, 0, 4, 4, W) if NP >= 256 else cut(sb("o_buf", [P, 4096]), 0, 4, 4, W)
        big = reg1 if NP >= 256 else sb("p2_buf", [P, 7168])
        a = a if NP >= 256 else 0
        v_t, a = cut(big, a, 512)
        v_h = half_words(big[:, a:a + 512], 2)
        v_m = half_words(big[:, a + 512:a + 768], 1)
        v_1 = half_words(big[:, a + 768:a + 1280], 2)
        v_2 = half_words(big[:, a + 1280:a + 1792], 2)
        ey = big[:, a + 1792:a + 2048].bitcast(bf16).rearrange("p (i w) -> p i w", i=2)
        a += 2048
        xt_sb, a = cut(big, a, 2, 2, 512)
        wr, a = cut(big, a, 2, 2, P)
        wp, a = cut(big, a, 2, 2, P)
        cs, a = cut(big, a, 4, 3, KW)

        names = """tab_in beta_in beta_zero
            x_in0 x_in1 x_in2 x_in3 x_used0 x_used1 x_used2 x_used3 gram_mm gram_copied sum_made diff_made xh_mm xh_copied xw_made xt_mm xt_copied dt_mm dt_copied d_mm d_copied
            xh_out0 xh_out1 gram_out diag_done dve_chain act_chain pool_chain
            spectra_ready stat_mm rot_mm rot_read root_wanted root_done ps_stored
            modes_in_in0 modes_in_in1 weights_in0 weights_in1 weights_ready modes_ready mode_mm mode_act mode_dve conv_stored0 conv_stored1 conv_in
            rot2_mm rot2_act c_ready m1_mm var_base var_prod var_ready var_mm r1_ready
            crs_in00 crs_in01 crs_in10 crs_in11 gram_in0 gram_in1 cr_ready q_half q_mm q_read gram_used
            qacc_ready qt_mm qt_ready r_mm r_ready cov_mm cov_ready cov_stored aug_in inv_ready inv_stored whit_zero whit_in
            ms_mm ms_ready mw_mm mw_ready
            cs_ready w_scaled w_ready x_re_in0 x_re_in1 x_re_in2 x_re_in3 v_mm ey_in ey_ready v_high v_rest v_mid v_split xt2_mm xt2_copied o_mm o_ready x_re_used0 x_re_used1 x_re_used2 x_re_used3
            out_stored0 out_stored1 out_stored2 out_stored3""".split()
        HEAD = dict(sync={},
                    tensor=dict(x_used0=1, x_used1=1, x_used2=1, x_used3=1, q_half=2, q_mm=2, v_mm=4, xt2_mm=4, o_mm=4,
                                x_re_used0=1, x_re_used1=1, x_re_used2=1, x_re_used3=1, xh_mm=2),
                    scalar=dict(ps_stored=1, dt_copied=1, xh_copied=2, gram_copied=2, rot2_act=4, xt2_copied=2, xh_out0=1,
                                xh_out1=1, gram_out=1, out_stored0=1, out_stored1=1, out_stored2=1, out_stored3=1),
                    vector=dict(xw_made=5, v_split=2, xt_copied=2, d_copied=1, diag_done=1, rot_read=1, q_read=2, o_ready=4),
                    gpsimd=dict(gram_used=2, w_ready=2))
        START = {name: k for starts in HEAD.values() for name, k in starts.items()}
        S = {n: sem(n) for n in names}

        def nth(name, n):
            return S[name], START.get(name, 0) + n

        def head_start(eng, which):
            for name, k in HEAD[which].items():
                eng.sem_inc(S[name], k)

        block = ctx.enter_context(nc.Block())

        @block.sync
        def _(sp):
            head_start(sp, "sync")
            sp.dma_start(tab[:, :], table[:, 0:ncols]).then_inc(S["tab_in"], 16)
            sp.wait_ge(*nth("beta_zero", 1))
            for c in range(2):
                sp.dma_start(beta[KX * c:KX * c + 1, :],
                             bias.rearrange("(n c) a b -> c (n a b)", c=2)[c:c + 1, :],
                             allow_slow_non_contiguous=True).then_inc(S["beta_in"], 16)
            def loads(u):
                for j in range(4):
                    sp.wait_ge(*nth(f"x_used{j}", u))
                    sp.dma_start(x_in[:, 4 * j:4 * j + 4], x_v[:, ds(u * HC + 4 * j, 4)]).then_inc(S[f"x_in{j}"], 16)

            def weights_load(h):
                for g in range(KG):
                    for s in range(2):
                        for r in range(2):
                            row = 32 * g + HC * s
                            sp.dma_start(weights[row:row + HC, h % 2, r],
                                         (w_re, w_im)[(s + r) % 2][h, :, :, KA * g:KA * g + KA, 0:KY].rearrange(
                                             "i o k y -> i o (k y)")).then_inc(S[f"weights_in{h % 2}"], 16)

            loads(0)
            weights_load(0)
            weights_load(1)
            with sp.Fori(1, NU) as u:
                loads(u)
            def modes_load(h):
                for g in range(KG):
                    sp.dma_start(modes_in[32 * g:32 * g + 32, h % 2],
                                 spec_d[:, :, :, h:NU:HEADS, KA * g:KA * g + KA].rearrange(
                                     "s n c b k y -> (s n c) b (k y)")).then_inc(S[f"modes_in_in{h % 2}"], 16)

            def conv_store(h, part):
                sp.wait_ge(*nth("mode_act", h * 2 * KA + KA * (part + 1)))
                sp.wait_ge(*nth("mode_dve", h * 2 * KA + KA * (part + 1)))
                for g in range(KG):
                    kx = KA * g + KA // 2 * part
                    sp.dma_start(conv_d[h, :, :, :, kx:kx + KA // 2].rearrange("b r c k n y -> b (r c) (k n y)"),
                                 modes_out[32 * g:32 * g + B, :, KA // 2 * part:KA // 2 * part + KA // 2].rearrange(
                                     "p c k n y -> p c (k n y)")).then_inc(S[f"conv_stored{part}"], 16)

            def conv_load(h):
                for part in range(2):
                    sp.wait_ge(*nth(f"conv_stored{part}", (h + 1) * (16 * KG)))
                for par in range(2):
                    for c in range(2):
                        for r in range(2):
                            row = KH * par + KX * c + NI * r
                            sp.dma_start(CT[row:row + NI, :, h].rearrange("p b c k -> p b (c k)"),
                                         conv_d[h, :, r, c, par:KX:2].rearrange("b k n y -> k b (n y)")
                                         ).then_inc(S["conv_in"], 16)

            sp.wait_ge(*nth("ps_stored", 16 * 8 * NU))
            modes_load(0)
            modes_load(1)
            for n in ("xh_out0", "xh_out1", "gram_out"):
                sp.wait_ge(*nth(n, 16 * NU))
            for h in range(HEADS):
                if 1 <= h < HEADS - 1:
                    sp.wait_ge(*nth("mode_mm", h * 2 * KA))
                    weights_load(h + 1)
                    modes_load(h + 1)
                if h >= 1:
                    conv_load(h - 1)
                for part in range(2):
                    conv_store(h, part)
            conv_load(HEADS - 1)
            sp.wait_ge(*nth("c_ready", 1))
            sp.dma_start(ey_f, table[:, ncols:ncols + 2 * W]).then_inc(S["ey_in"], 16)
            sp.wait_ge(*nth("var_ready", 1))
            with sp.Fori(0, NU // 2) as t:
                for e in range(2):
                    for part in range(2):
                        sp.wait_ge(*nth(("q_half", "q_mm")[part], t * 2 + e - 1))
                        n = slice(4 * part, 4 * part + 4)
                        sp.dma_start(crs[:, e, n, 0:W],
                                     xh_d[ds(t * 2 + e, 1), :, n].rearrange("u p a w -> (u p) a w")
                                     ).then_inc(S[f"crs_in{e}{part}"], 16)
                    sp.wait_ge(*nth("gram_used", t * 2 + e - 1))
                    sp.dma_start(gram_in[:, e], gram_d[ds(t * 2 + e, 1)].rearrange("u p a -> (u p) a")
                                 ).then_inc(S[f"gram_in{e}"], 16)
            sp.wait_ge(*nth("cov_ready", 1))
            sp.dma_start(cov_d.rearrange("p a b -> p (a b)"), cov[:, :]).then_inc(S["cov_stored"], 16)
            sp.wait_ge(*nth("cov_stored", 16))
            for half in range(2):
                for s in range(2):
                    g = 8 * half + 4 * s
                    sp.dma_start(aug[g:g + 4, :, 0:M],
                                 cov_d.rearrange("(q s m) f b -> s f q m b", q=4, s=2)[s, half, :, :, M * s:M * s + M]
                                 ).then_inc(S["aug_in"], 16)
            sp.wait_ge(*nth("inv_ready", 1))
            sp.dma_start(inv_d, inv[:, :, :]).then_inc(S["inv_stored"], 16)
            sp.wait_ge(*nth("inv_stored", 16))
            sp.wait_ge(*nth("whit_zero", 1))
            for half in range(2):
                for s in range(2):
                    for q in range(4):
                        g = 8 * half + 4 * s + q
                        row = BL * q + M * s
                        sp.dma_start(whit[row:row + M, half, row:row + M], inv_d[g]).then_inc(S["whit_in"], 16)
            sp.wait_ge(*nth("ms_ready", 1))
            def load(t, j):
                sp.dma_start(x_re[:, 2 * j:2 * j + 2], x_v[:, ds(t * 8 + 2 * j, 2)]).then_inc(S[f"x_re_in{j}"], 16)

            def store(t, j):
                sp.wait_ge(*nth("o_ready", t * 8 + 2 * j + 2))
                sp.dma_start(out_v[:, ds(t * 8 + 2 * j, 2)],
                             o_sb[:, j].rearrange("p (c r) w -> p c r w", c=2)).then_inc(S[f"out_stored{j}"], 16)

            for j in range(4):
                load(0, j)
            with sp.Fori(1, NP // 4) as t:
                for j in range(4):
                    sp.wait_ge(*nth(f"x_re_used{j}", t))
                    load(t, j)
                    store(t - 1, j)
            for j in range(4):
                store(NP // 4 - 1, j)
            for j in range(4):
                sp.wait_ge(*nth(f"out_stored{j}", 16 * (NP // 4)))

        @block.tensor
        def _(pe):
            head_start(pe, "tensor")
            mm = nc.tensor.matmul
            pe.wait_ge(*nth("tab_in", 16))
            one = dict(start=True, stop=True)

            def products(u, q):
                if q % 2 == 0:
                    pe.wait_ge(*nth(f"x_in{q // 2}", u * 16 + 16))
                    pe.wait_ge(*nth("gram_copied", u * 4 + q // 2 - 1))
                for half in range(2):
                    for c in range(2):
                        for t in range(2):
                            blk = x_in[:, 2 * q + c, t, P * half:P * half + P]
                            at = W * (q % 2) + P * half
                            ins = mm(bank[q // 2 % 2][:, at:at + P], blk, blk, start=c == 0 and t == 0 and half == 0,
                                     stop=c == 1 and t == 1, skip_group_check=True)
                if q % 2 == 1:
                    ins.then_inc(S["gram_mm"], 1)
                pe.wait_ge(*nth("xh_copied", u * PAIRS + q - 1))
                pe.wait_ge(*nth("sum_made", u * PAIRS + q + 1))
                pe.wait_ge(*nth("diff_made", u * PAIRS + q + 1))
                for par in range(2):
                    for c in range(2):
                        row = KH * par + KX * c
                        ins = mm(bank[2 + q % 2][row:row + KX, 0:W], hc[:, par], halves[:, q % 2, par, c], **one)
                ins.then_inc(S["xh_mm"], 1)

            def transposes(u, q):
                pe.wait_ge(*nth("xt_copied", u * PAIRS + q - 1))
                pe.wait_ge(*nth("xw_made", u * PAIRS + q + 1))
                for par in range(2):
                    ins = mm(bank[4 + q % 2][:, P * par:P * par + P], xw[:, q % 2, par], T("eye"),
                             start=par == 0, stop=True, is_transpose=True, skip_group_check=True)
                    if q % 2 == 0 and par == 0:
                        ins.then_inc(S[f"x_used{q // 2}"], 1)
                ins.then_inc(S["xt_mm"], 1)

            def spectra(u, i):
                pe.wait_ge(*nth("xt_copied", u * PAIRS + 2 * i + 2))
                pe.wait_ge(*nth("dt_copied", u * 4 + i))
                if i == 1:
                    pe.wait_ge(*nth("rot_read", u))
                for e in range(2):
                    for par in range(2):
                        row = BL * (2 * e + par)
                        ins = mm(bank[7][row:row + BL, 0:P], ew[:, par], xht[:, (2 * i + e) % 4, par], **one)
                ins.then_inc(S["dt_mm"], 1)

            def spectra_back(u, i):
                pe.wait_ge(*nth("dt_copied", u * 4 + i + 1))
                if i == 0:
                    pe.wait_ge(*nth("d_copied", u))
                ins = mm(bank[6][:, P * i:P * i + P], dt, T("eye"), start=i == 0, stop=True, is_transpose=True,
                         skip_group_check=True)
                if i == 3:
                    ins.then_inc(S["d_mm"], 1)

            def turned(u):
                pe.wait_ge(*nth("d_copied", u + 1))
                pe.wait_ge(*nth("rot_read", u))
                mm(bank[7][:, 0:PAIRS * KY].rearrange("p (n y) -> p n y", y=KY), T("rot"),
                   D[:, ds(u * PAIRS, PAIRS), KY:KW], **one).then_inc(S["rot_mm"], 1)

            def unit(u, first=False):
                for q in range(PAIRS):
                    products(u, q)
                    if q >= 1:
                        transposes(u, q - 1)
                    elif not first:
                        transposes(u - 1, PAIRS - 1)
                    stage = spectra if q % 2 else spectra_back
                    i = (q - 3) // 2 if q % 2 else (q - 4) // 2
                    if i >= 0:
                        stage(u, i)
                    elif not first:
                        stage(u - 1, i + 4)
                    if q == 4 and not first:
                        turned(u - 1)

            unit(0, first=True)
            with pe.Fori(1, NU) as u:
                unit(u)
            transposes(NU - 1, PAIRS - 1)
            spectra_back(NU - 1, 2)
            spectra(NU - 1, 3)
            spectra_back(NU - 1, 3)
            turned(NU - 1)
            pe.wait_ge(*nth("spectra_ready", 1))
            mm(bank[0][:, 0:NP], T("mean"), D[:, :, 0], **one).then_inc(S["stat_mm"], 1)
            mm(bank[1][:, 0:NP], T("ones"), ssq_part[:, :], **one).then_inc(S["stat_mm"], 1)
            for h in range(HEADS):
                pe.wait_ge(*nth("modes_ready", h + 1))
                pe.wait_ge(*nth("weights_ready", h + 1))
                for a in range(KA):
                    for part, (y0, y1) in enumerate(((0, 9), (9, KY))):
                        n = h * 2 * KA + 2 * a + part
                        if n >= 2:
                            pe.wait_ge(*nth("mode_act", n - 1))
                            pe.wait_ge(*nth("mode_dve", n - 1))
                        for y in range(y0, y1):
                            for g in range(KG):
                                r = slice(32 * g, 32 * g + 32)
                                ins = mm(bank[2 * g + part][32 * g:32 * g + B, 32 * (y - y0):32 * (y - y0) + 32],
                                         modes_in[r, h % 2, :, KY * a + y],
                                         weights[r, h % 2, :, :, KY * a + y].rearrange("p r (n c) -> p r c n", c=2), **one)
                        ins.then_inc(S["mode_mm"], 1)
            pe.wait_ge(*nth("conv_in", 16 * 8 * HEADS))
            with pe.Fori(0, NP // 64) as t:
                for e in range(4):
                    pe.wait_ge(*nth("rot2_act", t * 4 + e - 3))
                    mm(bank[2 + e][:, 0:16 * KY], T("rot"),
                       CTf[:, ds(t * 64 + 16 * e, 16)].rearrange("p n y -> p (n y)"), **one).then_inc(S["rot2_mm"], 1)
            pe.wait_ge(*nth("c_ready", 1))
            mm(bank[0][:, 0:NP], T("mean"), C[:, :, 0], **one).then_inc(S["m1_mm"], 1)
            pe.wait_ge(*nth("var_ready", 1))
            mm(bank[1][:, 0:NP], T("ones"), tmp[:, :], **one).then_inc(S["var_mm"], 1)
            with pe.Fori(0, NU // 2) as t:
                for e in range(2):
                    pe.wait_ge(*nth("cr_ready", t * 2 + e + 1))
                    pe.wait_ge(*nth("q_read", t * 2 + e - 1))
                    for q in range(PAIRS):
                        if q % 4 == 0:
                            pe.wait_ge(*nth(f"crs_in{e}{q // 4}", t * 16 + 16))
                        c = q % 2
                        ins = mm(bank[2 + e][KH * c:KH * c + KH, 0:W + KW], cr[:, e, q], crs[:, e, q],
                                 start=q < 2, stop=q >= PAIRS - 2)
                        if q == 3:
                            ins.then_inc(S["q_half"], 1)
                    ins.then_inc(S["q_mm"], 1)
            pe.wait_ge(*nth("qacc_ready", 1))
            nc.tensor.transpose(bank[0][0:KW, 0:P], qacc[:, W:W + KW], T("eye")).then_inc(S["qt_mm"], 1)
            pe.wait_ge(*nth("qt_ready", 1))
            mm(bank[1][0:KW + 1, 0:W], T("fold"), qacc[:, 0:W], start=True, stop=False)
            mm(bank[1][0:KW + 1, 0:W], qt[:, :], T("e0", KW), start=False, stop=True).then_inc(S["r_mm"], 1)
            pe.wait_ge(*nth("r_ready", 1))
            for half in range(2):
                for j in range(4):
                    w0 = P * half + BL * j
                    dst = bank[2][BL * j:BL * j + BL, BL * half:BL * half + BL]
                    e1 = T("e1", KW + 1)[:, w0:w0 + BL]
                    mm(dst, R[:, w0:w0 + BL], e1, start=half == 0, stop=False, skip_group_check=True)
                    mm(dst, e1, R[:, w0:w0 + BL], start=False, stop=False, skip_group_check=True)
                    ins = mm(dst, sneg[0:1, w0:w0 + BL], R[0:1, w0:w0 + BL], start=False, stop=True,
                             skip_group_check=True)
            ins.then_inc(S["cov_mm"], 1)
            for half in range(2):
                ins = mm(bank[3][:, P * half:P * half + P], R[0:1, P * half:P * half + P], T("ones", 1), start=half == 0,
                         stop=True, skip_group_check=True)
            ins.then_inc(S["ms_mm"], 1)
            pe.wait_ge(*nth("ms_ready", 1))
            pe.wait_ge(*nth("whit_in", 16 * 16))
            for half in range(2):
                ins = mm(bank[4][:, P * half:P * half + P], msum[:, half], whit[:, half], start=half == 0, stop=True,
                         skip_group_check=True)
            ins.then_inc(S["mw_mm"], 1)
            pe.wait_ge(*nth("mw_ready", 1))
            def expand(t, q):
                pe.wait_ge(*nth("cs_ready", t * 4 + q + 1))
                pe.wait_ge(*nth("v_split", t * 4 + q - 1))
                mm(bank[q % 2][0:3 * KW, :], cs[:, q].rearrange("p a b -> p (a b)"), T("hb"),
                   **one).then_inc(S["v_mm"], 1)

            def turn(t, q):
                pe.wait_ge(*nth(f"x_re_in{q}", t * 16 + 16))
                for half in range(2):
                    pe.wait_ge(*nth("xt2_copied", t * 8 + 2 * q + half - 1))
                    for c in range(2):
                        for r in range(2):
                            mm(bank[2 + half][:, H * c + P * r:H * c + P * r + P],
                               x_re[:, 2 * q + c, r, P * half:P * half + P], T("eye"), start=c == 0 and r == 0,
                               stop=False, is_transpose=True, skip_group_check=True)
                    pe.wait_ge(*nth("v_split", t * 4 + q + 1))
                    cols = slice(P * half, P * half + P)
                    mm(bank[2 + half][:, :], ey[0:3 * KW, 0, cols], v_1[0:3 * KW, q % 2],
                       start=False, stop=False, skip_group_check=True)
                    mm(bank[2 + half][:, :], ey[0:3 * KW, 1, cols], v_2[0:3 * KW, q % 2],
                       start=False, stop=True, skip_group_check=True).then_inc(S["xt2_mm"], 1)

            def whitened(t, q):
                e = q % 2
                pe.wait_ge(*nth("w_ready", t * 4 + q + 1))
                pe.wait_ge(*nth("xt2_copied", t * 8 + 2 * q + 2))
                for c in range(2):
                    pe.wait_ge(*nth("o_ready", t * 8 + 2 * q + c - 3))
                    for r in range(2):
                        for half in range(2):
                            ins = mm(bank[4 + 2 * e + c][:, W * r + P * half:W * r + P * half + P],
                                     xt_sb[:, e, half, H * c + P * r:H * c + P * r + P], wp[:, e, half],
                                     start=r == 0 and half == 0, stop=True, skip_group_check=True)
                            if c == 0 and r == 0 and half == 0:
                                ins.then_inc(S[f"x_re_used{q}"], 1)
                    ins.then_inc(S["o_mm"], 1)

            def four(t, first=False, last=False):
                for q in range(4):
                    turn(t, q)
                    if q < 2:
                        expand(t, q + 2)
                    elif not last:
                        expand(t + 1, q - 2)
                    if q >= 1:
                        whitened(t, q - 1)
                    elif not first:
                        whitened(t - 1, 3)

            pe.wait_ge(*nth("ey_ready", 1))
            expand(0, 0)
            expand(0, 1)
            four(0, first=True)
            with pe.Fori(1, NP // 4 - 1) as t:
                four(t)
            four(NP // 4 - 1, last=True)
            whitened(NP // 4 - 1, 3)

        def root(act, n, a):
            act.wait_ge(*nth("root_wanted", n))
            nc.scalar.activation(root_out[0:a.shape[0], 0:a.shape[1]], a, ACT.Sqrt).then_inc(S["root_done"], 1)

        @block.scalar
        def _(act):
            head_start(act, "scalar")
            copy = lambda o, i, **k: nc.scalar.activation(o, i, ACT.Copy, **k)
            def spectra_out(u):
                act.wait_ge(*nth("rot_read", u + 1))
                for par in range(2):
                    for c in range(2):
                        for s in range(2):
                            row = KH * par + KX * c + NI * s
                            act.dma_start(spec_d[s, :, c, ds(u, 1), par:KX:2].rearrange("n u k y -> k (n u) y"),
                                          psu[row:row + NI]).then_inc(S["ps_stored"], 16)

            def spectra_kept(u, i):
                act.wait_ge(*nth("dt_mm", u * 4 + i + 1))
                copy(dt, bank[7][:, 0:P]).then_inc(S["dt_copied"], 1)

            def unit(u, first=False):
                for q in range(PAIRS):
                    if q == 7 and not first:
                        spectra_out(u - 1)
                    if q % 4 == 0:
                        act.wait_ge(*nth(f"xh_out{q // 4}", u * 16))
                        act.wait_ge(*nth("xw_made", u * PAIRS + q - 4))
                    act.wait_ge(*nth("xh_mm", u * PAIRS + q + 1))
                    copy(xh[:, q], bank[2 + q % 2][:, 0:W]).then_inc(S["xh_copied"], 1)
                    if q % 2 == 1:
                        j = q // 2
                        if j == 0:
                            act.wait_ge(*nth("gram_out", u * 16))
                            act.wait_ge(*nth("diag_done", u))
                        act.wait_ge(*nth("gram_mm", u * 4 + j + 1))
                        for i in range(4):
                            r = slice(BL * i, BL * i + BL)
                            ins = copy(gram[r, 2 * j:2 * j + 2].rearrange("p n (f b) -> p (n f) b", f=2),
                                       bank[j % 2][r, :].rearrange("p (n b) -> p n b", b=P)[:, :, BL * i:BL * i + BL])
                        ins.then_inc(S["gram_copied"], 1)
                        if q >= 3:
                            spectra_kept(u, j - 1)
                        elif not first:
                            spectra_kept(u - 1, 3)
                    if q % 4 == 3:
                        j = q // 4
                        act.wait_ge(*nth("xh_copied", u * PAIRS + q + 1))
                        act.dma_start(xh_d[ds(u, 1), :, 4 * j:4 * j + 4].rearrange("u p a w -> (u p) a w"),
                                      xh[:, 4 * j:4 * j + 4]).then_inc(S[f"xh_out{j}"], 16)
                act.wait_ge(*nth("gram_copied", u * 4 + 4))
                act.dma_start(gram_d[ds(u, 1)].rearrange("u p a -> (u p) a"),
                              flat(gram[:, :, :])).then_inc(S["gram_out"], 16)

            unit(0, first=True)
            with act.Fori(1, NU) as u:
                unit(u)
            spectra_kept(NU - 1, 3)
            spectra_out(NU - 1)
            root(act, 1, root_in[:, :])
            for h in range(HEADS):
                for a in range(KA):
                    if h >= 1 and a % 4 == 0:
                        act.wait_ge(*nth(f"conv_stored{a // 4}", h * (16 * KG)))
                    for part, (y0, y1) in enumerate(((0, 9), (9, KY))):
                        act.wait_ge(*nth("mode_mm", h * 2 * KA + 2 * a + part + 1))
                        for g in range(2):
                            ins = copy(modes_out[32 * g:32 * g + B, :, a, :, y0:y1],
                                       bank[2 * g + part][32 * g:32 * g + B, 0:32 * (y1 - y0)].rearrange(
                                           "p (y r n) -> p r n y", r=4, n=PAIRS))
                        ins.then_inc(S["mode_act"], 1)
            with act.Fori(0, NP // 64) as t:
                for e in range(4):
                    act.wait_ge(*nth("rot2_mm", t * 4 + e + 1))
                    copy(C[:, ds(t * 64 + 16 * e, 16), KY:KW],
                         bank[2 + e][:, 0:16 * KY].rearrange("p (n y) -> p n y", y=KY),
                         scale=-1.0).then_inc(S["rot2_act"], 1)
            root(act, 2, root_in[:, :])
            act.wait_ge(*nth("qt_mm", 1))
            copy(qtp[:, :], bank[0][0:KW, 0:P]).then_inc(S["act_chain"], 1)
            act.wait_ge(*nth("ms_mm", 1))
            copy(msum[:, :, :].rearrange("p a b -> p (a b)"), bank[3][:, 0:W]).then_inc(S["ms_ready"], 1)
            root(act, 3, root_in[0:M, 0:M])
            act.wait_ge(*nth("mw_mm", 1))
            copy(mwhit[:, :], bank[4][:, 0:W], scale=1.0 / ROWS).then_inc(S["mw_ready"], 1)
            def scaled(t, q):
                act.wait_ge(*nth("w_ready", t * 4 + q - 1))
                copy(wr[:, q % 2].rearrange("p a b -> p (a b)"), flat(whit[:, :, :]),
                     scale=r1[:, ds(t * 4 + q, 1)]).then_inc(S["w_scaled"], 1)

            def high(t, q):
                act.wait_ge(*nth("v_mm", t * 4 + q + 1))
                act.wait_ge(*nth("v_split", t * 4 + q - 1))
                copy(v_h[0:3 * KW, q % 2], bank[q % 2][0:3 * KW, :]).then_inc(S["v_high"], 1)

            def middle(t, q):
                act.wait_ge(*nth("v_rest", t * 4 + q + 1))
                copy(v_m[0:3 * KW, 0], v_t[0:3 * KW, :]).then_inc(S["v_mid"], 1)

            def four(t, last=False):
                for q in range(4):
                    act.wait_ge(*nth("o_mm", t * 8 + 2 * q - 2))
                    for half in range(2):
                        act.wait_ge(*nth("xt2_mm", t * 8 + 2 * q + half + 1))
                        copy(xt_sb[:, q % 2, half], bank[2 + half][:, :]).then_inc(S["xt2_copied"], 1)
                    if not (last and q == 3):
                        scaled(*((t, q + 1) if q < 3 else (t + 1, 0)))
                    if not (last and q >= 2):
                        n, m = (t, q + 2) if q < 2 else (t + 1, q - 2)
                        high(n, m)
                        middle(n, m)

            scaled(0, 0)
            for q in range(2):
                high(0, q)
                middle(0, q)
            with act.Fori(0, NP // 4 - 1) as t:
                four(t)
            four(NP // 4 - 1, last=True)

        @block.gpsimd
        def _(pool):
            head_start(pool, "gpsimd")
            pch = Chain(pool, S["pool_chain"])
            pch(nc.gpsimd.memset(beta[:, :], 0.0))
            pool.sem_inc(S["beta_zero"], 1)
            pch(nc.gpsimd.memset(whit[:, :, :], 0.0))
            pool.sem_inc(S["whit_zero"], 1)
            with pool.Fori(0, NU) as u:
                for q in range(PAIRS):
                    if q % 2 == 0:
                        pool.wait_ge(*nth(f"x_in{q // 2}", u * 16 + 16))
                    pool.wait_ge(*nth("xh_mm", u * PAIRS + q - 1))
                    nc.gpsimd.tensor_tensor(out=halves[:, q % 2, 1], in0=x_in[:, 2 * q:2 * q + 2, 0],
                                            in1=x_in[:, 2 * q:2 * q + 2, 1],
                                            op=ALU.subtract).then_inc(S["diff_made"], 1)
            pool.wait_ge(*nth("tab_in", 16))
            for h in range(HEADS):
                pool.wait_ge(*nth(f"weights_in{h % 2}", (h // 2 + 1) * (16 * 4 * KG)))
                nc.gpsimd.tensor_scalar(weights[:, h % 2, 1], weights[:, h % 2, 1], T("sgn"), None,
                                        ALU.mult).then_inc(S["weights_ready"], 1)
                if h >= 1:
                    pool.wait_ge(*nth("modes_ready", h))
                    pool.wait_ge(*nth(f"modes_in_in{h % 2}", (h // 2 + 1) * 16 * KG))
                    mi = modes_in[:, h % 2]
                    pch(nc.gpsimd.tensor_tensor(out=mi[:, :, 0], in0=mi[:, :, 0], in1=m0_row[:, h:NU:HEADS],
                                                op=ALU.add))
                    nc.gpsimd.tensor_tensor(out=mi, in0=mi, in1=r0_row[:, h:NU:HEADS].unsqueeze(2).to_broadcast(
                        [P, B, KA * KY]), op=ALU.mult).then_inc(S["modes_ready"], 1)
            for i in range(NP // VN):
                pool.wait_ge(*nth("var_base", i + 1))
                nc.gpsimd.tensor_tensor(out=work[:, i % 2], in0=work[:, i % 2], in1=C[:, VN * i:VN * i + VN],
                                        op=ALU.mult).then_inc(S["var_prod"], 1)
            pool.wait_ge(*nth("r1_ready", 1))
            pch(nc.gpsimd.memset(gacc, 0.0))
            with pool.Fori(0, NU // 2) as t:
                pch.enter(t, 4)
                for e in range(2):
                    pool.wait_ge(*nth(f"gram_in{e}", t * 16 + 16))
                    g3 = lambda a: a.rearrange("p (n b) -> p n b", b=2 * BL)
                    pch(nc.gpsimd.tensor_tensor(
                        out=g3(gram_w), in0=g3(gram_in[:, e]),
                        in1=r1sq[:, ds((t * 2 + e) * PAIRS, PAIRS)].unsqueeze(2).to_broadcast([P, PAIRS, 2 * BL]),
                        op=ALU.mult))
                    pch(nc.gpsimd.tensor_tensor(out=gacc, in0=gacc, in1=gram_w, op=ALU.add))
                    pool.sem_inc(S["gram_used"], 1)
            pch.leave(NU // 2)
            pool.wait_ge(*nth("mw_ready", 1))
            pool.wait_ge(*nth("ey_in", 16))
            nc.gpsimd.tensor_copy(ey.rearrange("p i w -> p (i w)"), ey_f).then_inc(S["ey_ready"], 1)
            def spectrum_of(t, q):
                pool.wait_ge(*nth("v_mm", t * 4 + q - 3))
                nc.gpsimd.tensor_copy(cs[:, q], C[:, ds(t * 4 + q, 1)].to_broadcast([P, 3, KW])
                                      ).then_inc(S["cs_ready"], 1)

            def four(t, last=False):
                for q in range(4):
                    if not (last and q >= 2):
                        spectrum_of(*((t, q + 2) if q < 2 else (t + 1, q - 2)))
                    e = q % 2
                    pool.wait_ge(*nth("w_scaled", t * 4 + q + 1))
                    pool.wait_ge(*nth("o_mm", t * 8 + 2 * q - 2))
                    nc.gpsimd.tensor_tensor(out=wp[:, e], in0=wr[:, e],
                                            in1=T("eye").unsqueeze(1).to_broadcast([P, 2, P]),
                                            op=ALU.add).then_inc(S["w_ready"], 1)

            spectrum_of(0, 0)
            spectrum_of(0, 1)
            with pool.Fori(0, NP // 4 - 1) as t:
                four(t)
            four(NP // 4 - 1, last=True)

        @block.vector
        def _(dve):
            head_start(dve, "vector")
            v = nc.vector
            ch = Chain(dve, S["dve_chain"])

            def inverse_root(n, r, a):
                dve.sem_inc(S["root_wanted"], 1)
                dve.wait_ge(*nth("root_done", n))
                t = root_out[0:a.shape[0], 0:a.shape[1]]
                ch(v.reciprocal(r, t))
                ch(v.tensor_tensor(out=t, in0=r, in1=r, op=ALU.mult))
                ch(v.tensor_tensor(out=t, in0=t, in1=a, op=ALU.mult))
                ch(v.tensor_scalar(t, t, -0.5, 1.5, ALU.mult, ALU.add))
                ch(v.tensor_tensor(out=r, in0=r, in1=t, op=ALU.mult))

            dve.wait_ge(*nth("tab_in", 16))

            def halves_sum(u, q):
                if q % 2 == 0:
                    dve.wait_ge(*nth(f"x_in{q // 2}", u * 16 + 16))
                dve.wait_ge(*nth("xh_mm", u * PAIRS + q - 1))
                v.tensor_tensor(out=halves[:, q % 2, 0], in0=x_in[:, 2 * q:2 * q + 2, 0],
                                in1=x_in[:, 2 * q:2 * q + 2, 1], op=ALU.add).then_inc(S["sum_made"], 1)

            def width_halves(u, q):
                dve.wait_ge(*nth("xh_copied", u * PAIRS + q + 1))
                for par, op in enumerate((ALU.add, ALU.subtract)):
                    ins = v.tensor_tensor(out=xw[:, q % 2, par], in0=xh[:, q, 0:P], in1=xh[:, q, P:W], op=op)
                ins.then_inc(S["xw_made"], 1)

            def xt_copy(u, q):
                dve.wait_ge(*nth("xt_mm", u * PAIRS + q + 1))
                v.tensor_copy(xht[:, q % 4].rearrange("p a b -> p (a b)"),
                              bank[4 + q % 2][:, 0:W]).then_inc(S["xt_copied"], 1)

            def spectrum_kept(u):
                dve.wait_ge(*nth("d_mm", u + 1))
                for par in range(2):
                    ins = v.tensor_copy(
                        D[:, ds(u * PAIRS, PAIRS)].rearrange("p n (t k) -> p n t k", t=2)[:, :, :, par:KY:2],
                        bank[6][:, :].rearrange("p (n a t m) -> p n a t m", n=PAIRS, a=2, t=2)[
                            :, :, par, :, 0:(KY + 1 - par) // 2])
                ins.then_inc(S["d_copied"], 1)

            def diagonal(u):
                dve.wait_ge(*nth("gram_copied", u * 4 + 4))
                ch(v.tensor_tensor(out=gmask[:, :, :], in0=gram[:, :, :],
                                   in1=T("eye32").unsqueeze(1).to_broadcast([P, PAIRS, 2 * BL]), op=ALU.mult))
                dve.sem_inc(S["diag_done"], 1)

            def diagonal_sum(u):
                ch(v.tensor_reduce(out=ssq_part[:, ds(u * PAIRS, PAIRS)], in_=gmask[:, :, :], axis=AX.X, op=ALU.add))

            def unit(u, first=False):
                for q in range(PAIRS):
                    halves_sum(u, q)
                    before = (u, q - 1) if q >= 1 else (u - 1, PAIRS - 1)
                    if q >= 1 or not first:
                        width_halves(*before)
                    if q == 5 and not first:
                        turned(u - 1)
                    if q >= 1 or not first:
                        xt_copy(*before)
                    if not first:
                        if q == 0:
                            diagonal(u - 1)
                        elif q == 3:
                            spectrum_kept(u - 1)
                        elif q == 4:
                            diagonal_sum(u - 1)

            def turned(u):
                dve.wait_ge(*nth("rot_mm", u + 1))
                dve.wait_ge(*nth("ps_stored", 16 * 8 * u))
                v.tensor_tensor(out=psu[:, :, :], in0=bank[7][:, 0:PAIRS * KY].rearrange("p (n y) -> p n y", y=KY),
                                in1=D[:, ds(u * PAIRS, PAIRS), 0:KY], op=ALU.add).then_inc(S["rot_read"], 1)

            unit(0, first=True)
            with dve.Fori(1, NU) as u:
                ch.enter(u - 1, 2)
                unit(u)
            ch.leave(NU - 1)
            width_halves(NU - 1, PAIRS - 1)
            xt_copy(NU - 1, PAIRS - 1)
            diagonal(NU - 1)
            diagonal_sum(NU - 1)
            spectrum_kept(NU - 1)
            turned(NU - 1)
            dve.wait_ge(*nth("d_copied", NU))
            dve.sem_inc(S["spectra_ready"], 1)
            for n in ("xh_out0", "xh_out1", "gram_out"):
                dve.wait_ge(*nth(n, 16 * NU))
            dve.wait_ge(*nth("stat_mm", 2))
            ch(v.tensor_copy(m0[:, :], bank[0][:, 0:NP]))
            ch(v.tensor_copy(ssq[:, :], bank[1][:, 0:NP]))
            ch(v.tensor_tensor(out=tmp[:, :], in0=m0[:, :], in1=m0[:, :], op=ALU.mult))
            ch(v.scalar_tensor_tensor(out=r0[:, :], in0=ssq[:, :], scalar=1.0 / GROUP, in1=tmp[:, :],
                                      op0=ALU.mult, op1=ALU.subtract))
            ch(v.tensor_scalar(root_in[:, :], r0[:, :], EPS_GN, None, ALU.add))
            inverse_root(1, r0[:, :], root_in[:, :])
            for src, dst in ((m0[:, :], m0_row), (r0, r0_row)):
                ch(v.tensor_tensor(out=pick, in0=src.rearrange("p (u n) -> p u n", n=PAIRS),
                                   in1=T("pick").unsqueeze(1).to_broadcast([P, NU, PAIRS]), op=ALU.mult))
                ch(v.tensor_reduce(out=dst, in_=pick, axis=AX.X, op=ALU.add))
            ch(v.tensor_scalar(m0_row, m0_row, T("dcrow"), None, ALU.mult))

            dve.wait_ge(*nth("modes_in_in0", 16 * KG))
            mi = modes_in[:, 0]
            ch(v.tensor_tensor(out=mi[:, :, 0], in0=mi[:, :, 0], in1=m0_row[:, 0:NU:HEADS], op=ALU.add))
            ch(v.tensor_tensor(out=mi, in0=mi, in1=r0_row[:, 0:NU:HEADS].unsqueeze(2).to_broadcast(
                [P, B, KA * KY]), op=ALU.mult))
            dve.sem_inc(S["modes_ready"], 1)
            for h in range(HEADS):
                for a in range(KA):
                    if h >= 1 and a % 4 == 0:
                        dve.wait_ge(*nth(f"conv_stored{a // 4}", h * (16 * KG)))
                    for part, (y0, y1) in enumerate(((0, 9), (9, KY))):
                        dve.wait_ge(*nth("mode_mm", h * 2 * KA + 2 * a + part + 1))
                        for g in range(2, 4):
                            ins = v.tensor_copy(modes_out[32 * g:32 * g + B, :, a, :, y0:y1],
                                                bank[2 * g + part][32 * g:32 * g + B, 0:32 * (y1 - y0)].rearrange(
                                                    "p (y r n) -> p r n y", r=4, n=PAIRS))
                        ins.then_inc(S["mode_dve"], 1)
            dve.wait_ge(*nth("conv_in", 16 * 8 * HEADS))
            for part in range(2):
                dve.wait_ge(*nth(f"conv_stored{part}", HEADS * 16 * KG))
            ch(v.tensor_copy(C[:, :, 0:KY], CTf))
            dve.wait_ge(*nth("beta_in", 32))
            b0 = C[:, :, 0].rearrange("p (b n) -> p b n", n=HEADS * PAIRS)
            ch(v.scalar_tensor_tensor(out=b0, in0=beta[:, :].unsqueeze(1).to_broadcast([P, B, HEADS * PAIRS]),
                                      scalar=float(AREA), in1=b0, op0=ALU.mult, op1=ALU.add))
            dve.wait_ge(*nth("rot2_act", NP // 16))
            dve.sem_inc(S["c_ready"], 1)
            dve.wait_ge(*nth("m1_mm", 1))
            ch(v.tensor_tensor(out=m1[:, :], in0=bank[0][:, 0:NP], in1=m0[:, :], op=ALU.add))
            ch(v.tensor_scalar(tmp[:, :], m1[:, :], T("dc"), -float(AREA), ALU.mult, ALU.mult))
            ch(v.tensor_tensor(out=C[:, :, 0], in0=C[:, :, 0], in1=tmp[:, :], op=ALU.add))
            ch(v.memset(C[:, :, KY], 0.0))
            def var_sum(i):
                dve.wait_ge(*nth("var_prod", i + 1))
                ch(v.tensor_reduce(out=tmp[:, VN * i:VN * i + VN], in_=work[:, i % 2], axis=AX.X, op=ALU.add))
                ch(v.scalar_tensor_tensor(out=tmp[:, VN * i:VN * i + VN], in0=work[:, i % 2, :, 0], scalar=-0.5,
                                          in1=tmp[:, VN * i:VN * i + VN], op0=ALU.mult, op1=ALU.add))

            for i in range(NP // VN):
                s = slice(VN * i, VN * i + VN)
                ch(v.scalar_tensor_tensor(out=work[:, i % 2], in0=C[:, s], scalar=T("hk"), in1=D[:, s],
                                          op0=ALU.mult, op1=ALU.add))
                dve.sem_inc(S["var_base"], 1)
                if i >= 1:
                    var_sum(i - 1)
            var_sum(NP // VN - 1)
            dve.sem_inc(S["var_ready"], 1)
            dve.wait_ge(*nth("var_mm", 1))
            ch(v.scalar_tensor_tensor(out=r1[:, :], in0=bank[1][:, 0:NP], scalar=4.0 / AREA, in1=ssq[:, :],
                                      op0=ALU.mult, op1=ALU.add))
            ch(v.tensor_scalar(root_in[:, :], r1[:, :], 1.0 / GROUP, EPS_GN, ALU.mult, ALU.add))
            inverse_root(2, r1[:, :], root_in[:, :])
            ch(v.tensor_tensor(out=r1sq[:, :], in0=r1[:, :], in1=r1[:, :], op=ALU.mult))
            ch(v.memset(qacc, 0.0))
            ch(v.memset(cr.rearrange("p a b c -> p (a b c)"), 0.0))
            dve.sem_inc(S["r1_ready"], 1)
            def operands(u, e):
                n = ds(u * PAIRS, PAIRS)
                dve.wait_ge(*nth("q_mm", u - 1))
                ch(v.tensor_scalar(crs[:, e, :, W:W + KW], C[:, n], T("hh"), None, ALU.mult))
                ch(v.tensor_tensor(out=cr[:, e, :, 1:KW + 1], in0=C[:, n],
                                   in1=r1sq[:, n].unsqueeze(2).to_broadcast([P, PAIRS, KW]), op=ALU.mult))
                ch(v.tensor_scalar(cr[:, e, :, 0], r1[:, n], T("dc"), None, ALU.mult))
                dve.sem_inc(S["cr_ready"], 1)

            def accumulate(u, e):
                dve.wait_ge(*nth("q_mm", u + 1))
                ch(v.tensor_tensor(out=qacc, in0=bank[2 + e][:, 0:W + KW], in1=qacc, op=ALU.add))
                dve.sem_inc(S["q_read"], 1)

            operands(0, 0)
            with dve.Fori(0, NU // 2 - 1) as t:
                ch.enter(t, 8)
                operands(t * 2 + 1, 1)
                accumulate(t * 2, 0)
                operands(t * 2 + 2, 0)
                accumulate(t * 2 + 1, 1)
            ch.leave(NU // 2 - 1)
            operands(NU - 1, 1)
            accumulate(NU - 2, 0)
            accumulate(NU - 1, 1)
            dve.sem_inc(S["qacc_ready"], 1)
            dve.wait_ge(*nth("act_chain", 1))
            ch(v.tensor_tensor(out=qt[:, :], in0=qtp[:, 0:KW + 1], in1=qtp[:, KH:KH + KW + 1], op=ALU.add))
            ch(v.tensor_scalar(qt[:, 0:1], qt[:, 0:1], 2.0, None, ALU.mult))
            dve.sem_inc(S["qt_ready"], 1)
            dve.wait_ge(*nth("r_mm", 1))
            ch(v.tensor_copy(R[:, :], bank[1][0:KW + 1, 0:W]))
            ch(v.tensor_scalar(sneg[:, :], R[0:1, :], -1.0 / ROWS, None, ALU.mult))
            dve.sem_inc(S["r_ready"], 1)
            dve.wait_ge(*nth("gram_used", NU))
            ch(v.tensor_reduce(out=covg[:, :], in_=gacc.rearrange("p (n b) -> p b n", b=2 * BL), axis=AX.X,
                               op=ALU.add))
            dve.wait_ge(*nth("cov_mm", 1))
            ch(v.tensor_tensor(out=cov[:, :], in0=bank[2][:, 0:2 * BL], in1=covg[:, :], op=ALU.add))
            ch(v.tensor_scalar(cov[:, :], cov[:, :], (1.0 - EPS_W) / DENOM / DENOM, None, ALU.mult))
            ch(v.scalar_tensor_tensor(out=cov[:, :], in0=T("eye32"), scalar=EPS_W / DENOM, in1=cov[:, :],
                                      op0=ALU.mult, op1=ALU.add))
            dve.sem_inc(S["cov_ready"], 1)
            ch(v.memset(aug[:, :, M:2 * M], 0.0))
            diag = aug[:, :, :].rearrange("p a b -> p (a b)")
            ch(v.memset(diag[:, M:M + (2 * M + 1) * (M - 1) + 1:2 * M + 1], 1.0))
            dve.wait_ge(*nth("aug_in", 16 * 4))
            for j in range(M - 1):
                n = M - 1 - j
                ch(v.reciprocal(fac[:, 0:1], aug[:, j, j:j + 1]))
                ch(v.tensor_scalar(fac[:, 1:1 + n], aug[:, j + 1:M, j], fac[:, 0:1], None, ALU.mult))
                ch(v.tensor_tensor(out=step_[:, 0:n], in0=aug[:, j, :].unsqueeze(1).to_broadcast([M, n, 2 * M]),
                                   in1=fac[:, 1:1 + n].unsqueeze(2).to_broadcast([M, n, 2 * M]), op=ALU.mult))
                ch(v.tensor_tensor(out=aug[:, j + 1:M], in0=aug[:, j + 1:M], in1=step_[:, 0:n], op=ALU.subtract))
            ch(v.tensor_copy(root_in[0:M, 0:M], diag[:, 0:(2 * M + 1) * (M - 1) + 1:2 * M + 1]))
            inverse_root(3, fac[:, :], root_in[0:M, 0:M])
            ch(v.tensor_tensor(out=inv[:, :, :], in0=aug[:, :, M:2 * M].rearrange("p m k -> p k m"),
                               in1=fac[:, :].unsqueeze(1).to_broadcast([M, M, M]), op=ALU.mult))
            dve.sem_inc(S["inv_ready"], 1)
            dve.wait_ge(*nth("mw_ready", 1))
            def split(t, q):
                e, r = q % 2, slice(0, 3 * KW)
                n = t * 4 + q
                dve.wait_ge(*nth("v_high", n + 1))
                dve.wait_ge(*nth("v_split", n))
                v.scalar_tensor_tensor(out=v_t[r], in0=v_h[r, e], scalar=T("cut1", 3 * KW), in1=bank[e][r, :],
                                       op0=ALU.mult, op1=ALU.add).then_inc(S["v_rest"], 1)
                dve.wait_ge(*nth("xt2_mm", 2 * n - 2))
                v.scalar_tensor_tensor(out=v_2[r, e], in0=v_h[r, e], scalar=T("cut2", 3 * KW), in1=bank[e][r, :],
                                       op0=ALU.mult, op1=ALU.add)
                dve.wait_ge(*nth("v_mid", n + 1))
                v.scalar_tensor_tensor(out=v_1[r, e], in0=v_m[r, 0], scalar=T("cut2", 3 * KW), in1=v_t[r],
                                       op0=ALU.mult, op1=ALU.add).then_inc(S["v_split"], 1)

            def result(t, q):
                dve.wait_ge(*nth(f"out_stored{q}", t * 16))
                for c in range(2):
                    dve.wait_ge(*nth("o_mm", t * 8 + 2 * q + c + 1))
                    v.scalar_tensor_tensor(
                        out=o_sb[:, q, 2 * c:2 * c + 2],
                        in0=bank[4 + 2 * (q % 2) + c][:, :].rearrange("p (r w) -> p r w", r=2),
                        scalar=m1[:, ds(t * 4 + q, 1)],
                        in1=mwhit[:, :].unsqueeze(1).to_broadcast([P, 2, W]),
                        op0=ALU.add, op1=ALU.subtract).then_inc(S["o_ready"], 1)

            def four(t, first=False, last=False):
                for q in range(4):
                    if not (last and q >= 2):
                        split(*((t, q + 2) if q < 2 else (t + 1, q - 2)))
                    if q >= 1:
                        result(t, q - 1)
                    elif not first:
                        result(t - 1, 3)

            split(0, 0)
            split(0, 1)
            four(0, first=True)
            with dve.Fori(1, NP // 4 - 1) as t:
                four(t)
            four(NP // 4 - 1, last=True)
            result(NP // 4 - 1, 3)


_INS = ["x", "L0_conv_weight_re", "L0_conv_weight_im", "L0_conv_bias"]


def kernel(**inputs):
    import concourse.bacc as _bacc
    from concourse.bass_utils import run_bass_kernel_spmd as _run

    nc = _bacc.Bacc("TRN2", target_bir_lowering=False, num_devices=1)
    arrays, args = {}, []
    for name in _INS:
        a = np.ascontiguousarray(inputs[name])
        arrays[f"in_{name}_dram"] = a
        args.append(nc.dram_tensor(f"in_{name}_dram", a.shape, mybir.dt.from_np(a.dtype), kind="ExternalInput").ap())
    table = tables()
    arrays["table_dram"] = table
    args.append(nc.dram_tensor("table_dram", table.shape, mybir.dt.float32, kind="ExternalInput").ap())
    shape = tuple(inputs["x"].shape)
    args.append(nc.dram_tensor("out_0_dram", shape, mybir.dt.float32, kind="ExternalOutput").ap())
    whiten_kernel(nc, *args)
    r = _run(nc, [arrays], core_ids=[0])
    return r.results[0]["out_0_dram"]
```
